# Optimizing a Trainium2 kernel written in Bass

```python
import numpy as np
import jax
import jax.numpy as jnp

def _softmax(x, axis=-1):
    return jax.nn.softmax(x, axis=axis)

def _gelu(x):
    return jax.nn.gelu(x, approximate=True)

def _silu(x):
    return jax.nn.silu(x)

def _sigmoid(x):
    return jax.nn.sigmoid(x)

def _layernorm(x, axis=-1, eps=1e-05):
    m = jnp.mean(x, axis=axis, keepdims=True)
    v = jnp.var(x, axis=axis, keepdims=True)
    return (x - m) / jnp.sqrt(v + eps)

def _scatter_add(tgt, idx, src, axis=0):
    return tgt.at[idx].add(src)

def _segment_sum(src, seg, n):
    return jax.ops.segment_sum(src, seg, n)
kernel_name = 'mk_lm_tower_d2_tok_ids2048_r4_48239a'

def setup_inputs(seed: int=0):
    np.random.seed(seed)
    _w = jnp.asarray

    def _rec_inputs():
        import jax
        import jax.numpy as jnp
        _rk = jax.random.key(seed)
        x = jax.random.randint(jax.random.fold_in(_rk, 1), (8, 256), 0, 512, jnp.int32)
        return x
    x = _rec_inputs()

    def _L0_tok_setup():
        import jax, jax.numpy as jnp
        import numpy as np
        B, S, D, DQK, L = (4, 512, 512, 128, 4)

        def _sinusoidal_pe(seq_len, d_model):
            pos = jnp.arange(seq_len, dtype=jnp.float32)[:, None]
            half = jnp.arange(0, d_model, 2, dtype=jnp.float32)
            div = jnp.exp(-(jnp.log(jnp.float32(10000.0)) / d_model) * half)
            pe = jnp.zeros((seq_len, d_model), jnp.float32)
            pe = pe.at[:, 0::2].set(jnp.sin(pos * div))
            pe = pe.at[:, 1::2].set(jnp.cos(pos * div))
            return pe
        key = jax.random.key(seed)
        k1, k2, k3 = jax.random.split(key, 3)
        token_ids = jax.random.randint(k1, (B, S), 0, D)
        Wq = jax.random.normal(k2, (L, D, DQK), jnp.float32) * 0.02
        Wk = jax.random.normal(k3, (L, D, DQK), jnp.float32) * 0.02
        return {'token_ids': token_ids, 'Wq': Wq, 'Wk': Wk}
    _L0_tok_all = _L0_tok_setup()
    _L0_tok_in = {k: v for k, v in _L0_tok_all.items() if k in ('Wq', 'Wk')}
    del _L0_tok_all

    def _L0_attn_setup():
        import jax, jax.numpy as jnp
        import numpy as np
        HIDDEN = 512
        NUM_HEADS = 16
        HEAD_DIM = 128
        OUT = NUM_HEADS * HEAD_DIM
        B, T = (4, 512)

        def _wkv(r, k, v, time_decay, time_first):
            w = jnp.exp(-jnp.exp(time_decay))
            u = time_first
            kv = k * v
            r_t = jnp.moveaxis(r, 1, 0)
            kv_t = jnp.moveaxis(kv, 1, 0)

            def step(state, inp):
                rt, kvt = inp
                out = (state + u * kvt) * rt
                new_state = state * w + kvt
                return (new_state, out)
            state0 = jnp.zeros(r.shape[:1] + r.shape[2:], dtype=r.dtype)
            _, out = jax.lax.scan(step, state0, (r_t, kv_t))
            return jnp.moveaxis(out, 0, 1)
        key = jax.random.key(seed)
        ks = jax.random.split(key, 8)
        hidden_states = jax.random.normal(ks[0], (B, T, HIDDEN), dtype=jnp.float32)
        scale = 0.02
        Wr = jax.random.normal(ks[1], (OUT, HIDDEN), dtype=jnp.float32) * scale
        Wk = jax.random.normal(ks[2], (OUT, HIDDEN), dtype=jnp.float32) * scale
        Wv = jax.random.normal(ks[3], (OUT, HIDDEN), dtype=jnp.float32) * scale
        Wo = jax.random.normal(ks[4], (HIDDEN, OUT), dtype=jnp.float32) * scale
        time_decay = jax.random.uniform(ks[5], (NUM_HEADS, HEAD_DIM), minval=-4.0, maxval=-1.0, dtype=jnp.float32)
        time_first = jax.random.uniform(ks[6], (NUM_HEADS, HEAD_DIM), minval=-0.5, maxval=0.5, dtype=jnp.float32)
        time_mix_k = jnp.full((1, 1, HIDDEN), 0.5, dtype=jnp.float32)
        time_mix_v = jnp.full((1, 1, HIDDEN), 0.5, dtype=jnp.float32)
        time_mix_r = jnp.full((1, 1, HIDDEN), 0.5, dtype=jnp.float32)
        return {'hidden_states': hidden_states, 'Wr': Wr, 'Wk': Wk, 'Wv': Wv, 'Wo': Wo, 'time_decay': time_decay, 'time_first': time_first, 'time_mix_k': time_mix_k, 'time_mix_v': time_mix_v, 'time_mix_r': time_mix_r}
    _L0_attn_all = _L0_attn_setup()
    _L0_attn_in = {k: v for k, v in _L0_attn_all.items() if k in ('Wr', 'Wk', 'Wv', 'Wo', 'time_decay', 'time_first', 'time_mix_k', 'time_mix_v', 'time_mix_r')}
    del _L0_attn_all

    def _L0_ffn_setup():
        import jax, jax.numpy as jnp
        import numpy as np
        EPS = 1e-08

        def _bit_quant(w):
            scale = jnp.maximum(jnp.mean(jnp.abs(w)), EPS)
            w_ternary = jnp.clip(jnp.round(w / scale), -1.0, 1.0)
            return w + jax.lax.stop_gradient(w_ternary - w)
        key = jax.random.key(seed)
        k = jax.random.split(key, 5)
        emb, dff = (512, 2048)
        B, S = (4, 512)
        x = jax.random.normal(k[0], (B, S, emb), dtype=jnp.float32)
        w1 = jax.random.normal(k[1], (dff, emb), dtype=jnp.float32) * 0.02
        b1 = jax.random.normal(k[2], (dff,), dtype=jnp.float32) * 0.02
        w2 = jax.random.normal(k[3], (emb, dff), dtype=jnp.float32) * 0.02
        b2 = jax.random.normal(k[4], (emb,), dtype=jnp.float32) * 0.02
        return {'x': x, 'w1': w1, 'b1': b1, 'w2': w2, 'b2': b2}
    _L0_ffn_all = _L0_ffn_setup()
    _L0_ffn_in = {k: v for k, v in _L0_ffn_all.items() if k in ('w1', 'b1', 'w2', 'b2')}
    del _L0_ffn_all

    def _L1_attn_setup():
        import jax, jax.numpy as jnp
        import numpy as np
        H = 16
        D = 128
        HID = 512
        BLOCK = 64
        TOPK = 8

        def _moba_forward(hidden_states, Wq, Wk, Wv, Wo):
            B, S, _ = hidden_states.shape
            nb = S // BLOCK
            INF = jnp.float32(jnp.inf)
            q = (hidden_states @ Wq).reshape(B, S, H, D)
            k = (hidden_states @ Wk).reshape(B, S, H, D)
            v = (hidden_states @ Wv).reshape(B, S, H, D)
            kg = k.reshape(B, nb, BLOCK, H, D).mean(axis=2)
            gate = jnp.einsum('bshd,bnhd->bhsn', q, kg)
            pos = jnp.arange(S)
            qb = pos // BLOCK
            blk = jnp.arange(nb)
            is_self = qb[:, None] == blk[None, :]
            not_past = pos[:, None] < (blk[None, :] + 1) * BLOCK
            gate = jnp.where(is_self, INF, jnp.where(not_past, -INF, gate))
            kk = min(TOPK, nb)
            topv, topi = jax.lax.top_k(gate, kk)
            thresh = topv.min(axis=-1, keepdims=True)
            idx_mask = (topi[..., None] == blk).any(axis=-2)
            need = (gate >= thresh) & idx_mask
            gate_bias = jnp.where(need, 0.0, -INF)
            sm_scale = D ** (-0.5)
            qk = jnp.einsum('bshd,bthd->bhst', q, k) * sm_scale
            qk = qk.reshape(B, H, S, nb, BLOCK) + gate_bias[..., None]
            qk = qk.reshape(B, H, S, S)
            causal = pos[:, None] >= pos[None, :]
            qk = jnp.where(causal, qk, -INF)
            p = jax.nn.softmax(qk, axis=-1)
            o = jnp.einsum('bhst,bthd->bshd', p, v).reshape(B, S, H * D)
            return o @ Wo
        key = jax.random.key(seed)
        ks = jax.random.split(key, 5)
        B, S = (1, 512)
        hidden_states = jax.random.normal(ks[0], (B, S, HID), dtype=jnp.float32)
        scale = HID ** (-0.5)
        Wq = jax.random.normal(ks[1], (HID, H * D), dtype=jnp.float32) * scale
        Wk = jax.random.normal(ks[2], (HID, H * D), dtype=jnp.float32) * scale
        Wv = jax.random.normal(ks[3], (HID, H * D), dtype=jnp.float32) * scale
        Wo = jax.random.normal(ks[4], (H * D, HID), dtype=jnp.float32) * scale
        return {'hidden_states': hidden_states, 'Wq': Wq, 'Wk': Wk, 'Wv': Wv, 'Wo': Wo}
    _L1_attn_all = _L1_attn_setup()
    _L1_attn_in = {k: v for k, v in _L1_attn_all.items() if k in ('Wq', 'Wk', 'Wv', 'Wo')}
    del _L1_attn_all

    def _L1_ffn_setup():
        import jax, jax.numpy as jnp
        import numpy as np
        HIDDEN = 512
        INTER = 1376
        LUT_SIZE = 16

        def _ghost_linear(x, idx, lut):
            w = lut[idx]
            return jnp.einsum('bsh,oh->bso', x, w)
        key = jax.random.key(seed)
        k_x, k_lut, k_g, k_u, k_d = jax.random.split(key, 5)
        x = jax.random.normal(k_x, (2, 1024, HIDDEN), dtype=jnp.float32)
        lut = jax.random.normal(k_lut, (LUT_SIZE,), dtype=jnp.float32) * 0.02
        gate_idx = jax.random.randint(k_g, (INTER, HIDDEN), 0, LUT_SIZE, dtype=jnp.int32)
        up_idx = jax.random.randint(k_u, (INTER, HIDDEN), 0, LUT_SIZE, dtype=jnp.int32)
        down_idx = jax.random.randint(k_d, (HIDDEN, INTER), 0, LUT_SIZE, dtype=jnp.int32)
        return {'x': x, 'lut': lut, 'gate_idx': gate_idx, 'up_idx': up_idx, 'down_idx': down_idx}
    _L1_ffn_all = _L1_ffn_setup()
    _L1_ffn_in = {k: v for k, v in _L1_ffn_all.items() if k in ('lut', 'gate_idx', 'up_idx', 'down_idx')}
    del _L1_ffn_all
    return {'x': x, 'L0_tok_Wq': _L0_tok_in['Wq'], 'L0_tok_Wk': _L0_tok_in['Wk'], 'L0_attn_Wr': _L0_attn_in['Wr'], 'L0_attn_Wk': _L0_attn_in['Wk'], 'L0_attn_Wv': _L0_attn_in['Wv'], 'L0_attn_Wo': _L0_attn_in['Wo'], 'L0_attn_time_decay': _L0_attn_in['time_decay'], 'L0_attn_time_first': _L0_attn_in['time_first'], 'L0_attn_time_mix_k': _L0_attn_in['time_mix_k'], 'L0_attn_time_mix_v': _L0_attn_in['time_mix_v'], 'L0_attn_time_mix_r': _L0_attn_in['time_mix_r'], 'L0_ffn_w1': _L0_ffn_in['w1'], 'L0_ffn_b1': _L0_ffn_in['b1'], 'L0_ffn_w2': _L0_ffn_in['w2'], 'L0_ffn_b2': _L0_ffn_in['b2'], 'L1_attn_Wq': _L1_attn_in['Wq'], 'L1_attn_Wk': _L1_attn_in['Wk'], 'L1_attn_Wv': _L1_attn_in['Wv'], 'L1_attn_Wo': _L1_attn_in['Wo'], 'L1_ffn_lut': _L1_ffn_in['lut'], 'L1_ffn_gate_idx': _L1_ffn_in['gate_idx'], 'L1_ffn_up_idx': _L1_ffn_in['up_idx'], 'L1_ffn_down_idx': _L1_ffn_in['down_idx']}

def reference(x, L0_tok_Wq, L0_tok_Wk, L0_attn_Wr, L0_attn_Wk, L0_attn_Wv, L0_attn_Wo, L0_attn_time_decay, L0_attn_time_first, L0_attn_time_mix_k, L0_attn_time_mix_v, L0_attn_time_mix_r, L0_ffn_w1, L0_ffn_b1, L0_ffn_w2, L0_ffn_b2, L1_attn_Wq, L1_attn_Wk, L1_attn_Wv, L1_attn_Wo, L1_ffn_lut, L1_ffn_gate_idx, L1_ffn_up_idx, L1_ffn_down_idx):
    import jax
    import jax.numpy as jnp

    def _L0_tok_ref(token_ids, Wq, Wk):
        import jax, jax.numpy as jnp
        import numpy as np
        B, S, D, DQK, L = (4, 512, 512, 128, 4)

        def _sinusoidal_pe(seq_len, d_model):
            pos = jnp.arange(seq_len, dtype=jnp.float32)[:, None]
            half = jnp.arange(0, d_model, 2, dtype=jnp.float32)
            div = jnp.exp(-(jnp.log(jnp.float32(10000.0)) / d_model) * half)
            pe = jnp.zeros((seq_len, d_model), jnp.float32)
            pe = pe.at[:, 0::2].set(jnp.sin(pos * div))
            pe = pe.at[:, 1::2].set(jnp.cos(pos * div))
            return pe
        d_model = Wq.shape[1]
        d_qk = Wq.shape[2]
        seq_len = token_ids.shape[1]
        enc = jax.nn.one_hot(token_ids, d_model, dtype=jnp.float32)
        enc = enc + _sinusoidal_pe(seq_len, d_model)[None, :, :]
        causal_mask = jnp.triu(jnp.ones((seq_len, seq_len), bool), 1)
        scale = 1.0 / jnp.sqrt(jnp.float32(d_qk))

        def layer(enc, ws):
            wq, wk = ws
            q = enc @ wq
            k = enc @ wk
            sims = jnp.einsum('bqd,bkd->bqk', q, k) * scale
            sims = jnp.where(causal_mask[None, :, :], jnp.float32(-1000000000.0), sims)
            attn = jax.nn.softmax(sims, axis=-1)
            enc = jnp.einsum('bqk,bkd->bqd', attn, enc)
            return (enc, None)
        enc, _ = jax.lax.scan(layer, enc, (Wq, Wk))
        return enc

    def _L0_attn_ref(hidden_states, Wr, Wk, Wv, Wo, time_decay, time_first, time_mix_k, time_mix_v, time_mix_r):
        import jax, jax.numpy as jnp
        import numpy as np
        HIDDEN = 512
        NUM_HEADS = 16
        HEAD_DIM = 128
        OUT = NUM_HEADS * HEAD_DIM
        B, T = (4, 512)

        def _wkv(r, k, v, time_decay, time_first):
            w = jnp.exp(-jnp.exp(time_decay))
            u = time_first
            kv = k * v
            r_t = jnp.moveaxis(r, 1, 0)
            kv_t = jnp.moveaxis(kv, 1, 0)

            def step(state, inp):
                rt, kvt = inp
                out = (state + u * kvt) * rt
                new_state = state * w + kvt
                return (new_state, out)
            state0 = jnp.zeros(r.shape[:1] + r.shape[2:], dtype=r.dtype)
            _, out = jax.lax.scan(step, state0, (r_t, kv_t))
            return jnp.moveaxis(out, 0, 1)
        Bc, Tc, _ = hidden_states.shape
        xx = jnp.concatenate([jnp.zeros_like(hidden_states[:, :1]), hidden_states[:, :-1]], axis=1)
        xk = hidden_states * time_mix_k + xx * (1.0 - time_mix_k)
        xv = hidden_states * time_mix_v + xx * (1.0 - time_mix_v)
        xr = hidden_states * time_mix_r + xx * (1.0 - time_mix_r)
        receptance = jax.nn.sigmoid(jnp.einsum('bth,oh->bto', xr, Wr))
        key = jnp.einsum('bth,oh->bto', xk, Wk)
        value = jnp.einsum('bth,oh->bto', xv, Wv)
        receptance = receptance.reshape(Bc, Tc, NUM_HEADS, HEAD_DIM)
        key = key.reshape(Bc, Tc, NUM_HEADS, HEAD_DIM)
        value = value.reshape(Bc, Tc, NUM_HEADS, HEAD_DIM)
        wkv = _wkv(receptance, key, value, time_decay, time_first)
        attn = wkv.reshape(Bc, Tc, OUT)
        return jnp.einsum('bto,ho->bth', attn, Wo)

    def _L0_ffn_ref(x, w1, b1, w2, b2):
        import jax, jax.numpy as jnp
        import numpy as np
        EPS = 1e-08

        def _bit_quant(w):
            scale = jnp.maximum(jnp.mean(jnp.abs(w)), EPS)
            w_ternary = jnp.clip(jnp.round(w / scale), -1.0, 1.0)
            return w + jax.lax.stop_gradient(w_ternary - w)
        w1q = _bit_quant(w1)
        w2q = _bit_quant(w2)
        h = jnp.einsum('bsd,fd->bsf', x, w1q) + b1
        h = jax.nn.gelu(h, approximate=False)
        return jnp.einsum('bsf,df->bsd', h, w2q) + b2

    def _L1_attn_ref(hidden_states, Wq, Wk, Wv, Wo):
        import jax, jax.numpy as jnp
        import numpy as np
        H = 16
        D = 128
        HID = 512
        BLOCK = 64
        TOPK = 8

        def _moba_forward(hidden_states, Wq, Wk, Wv, Wo):
            B, S, _ = hidden_states.shape
            nb = S // BLOCK
            INF = jnp.float32(jnp.inf)
            q = (hidden_states @ Wq).reshape(B, S, H, D)
            k = (hidden_states @ Wk).reshape(B, S, H, D)
            v = (hidden_states @ Wv).reshape(B, S, H, D)
            kg = k.reshape(B, nb, BLOCK, H, D).mean(axis=2)
            gate = jnp.einsum('bshd,bnhd->bhsn', q, kg)
            pos = jnp.arange(S)
            qb = pos // BLOCK
            blk = jnp.arange(nb)
            is_self = qb[:, None] == blk[None, :]
            not_past = pos[:, None] < (blk[None, :] + 1) * BLOCK
            gate = jnp.where(is_self, INF, jnp.where(not_past, -INF, gate))
            kk = min(TOPK, nb)
            topv, topi = jax.lax.top_k(gate, kk)
            thresh = topv.min(axis=-1, keepdims=True)
            idx_mask = (topi[..., None] == blk).any(axis=-2)
            need = (gate >= thresh) & idx_mask
            gate_bias = jnp.where(need, 0.0, -INF)
            sm_scale = D ** (-0.5)
            qk = jnp.einsum('bshd,bthd->bhst', q, k) * sm_scale
            qk = qk.reshape(B, H, S, nb, BLOCK) + gate_bias[..., None]
            qk = qk.reshape(B, H, S, S)
            causal = pos[:, None] >= pos[None, :]
            qk = jnp.where(causal, qk, -INF)
            p = jax.nn.softmax(qk, axis=-1)
            o = jnp.einsum('bhst,bthd->bshd', p, v).reshape(B, S, H * D)
            return o @ Wo
        return _moba_forward(hidden_states, Wq, Wk, Wv, Wo)

    def _L1_ffn_ref(x, lut, gate_idx, up_idx, down_idx):
        import jax, jax.numpy as jnp
        import numpy as np
        HIDDEN = 512
        INTER = 1376
        LUT_SIZE = 16

        def _ghost_linear(x, idx, lut):
            w = lut[idx]
            return jnp.einsum('bsh,oh->bso', x, w)
        gate = _ghost_linear(x, gate_idx, lut)
        up = _ghost_linear(x, up_idx, lut)
        h = jax.nn.silu(gate) * up
        return _ghost_linear(h, down_idx, lut)
    h = _L0_tok_ref(x, L0_tok_Wq, L0_tok_Wk)
    h = h + _L0_attn_ref(_layernorm(h, axis=-1), L0_attn_Wr, L0_attn_Wk, L0_attn_Wv, L0_attn_Wo, L0_attn_time_decay, L0_attn_time_first, L0_attn_time_mix_k, L0_attn_time_mix_v, L0_attn_time_mix_r)
    h = h + _L0_ffn_ref(_layernorm(h, axis=-1), L0_ffn_w1, L0_ffn_b1, L0_ffn_w2, L0_ffn_b2)
    h = h + _L1_attn_ref(_layernorm(h, axis=-1), L1_attn_Wq, L1_attn_Wk, L1_attn_Wv, L1_attn_Wo)
    h = h + _L1_ffn_ref(_layernorm(h, axis=-1), L1_ffn_lut, L1_ffn_gate_idx, L1_ffn_up_idx, L1_ffn_down_idx)
    return h

_drawn_inputs = setup_inputs


def setup_inputs(seed=0):
    import zlib

    import numpy as np

    out = dict(_drawn_inputs(seed))
    spreads = {'L0_attn_time_mix_k': (0.5, 0.6),
     'L0_attn_time_mix_v': (0.5, 0.6),
     'L0_attn_time_mix_r': (0.5, 0.6)}
    factors = {'L0_tok_Wq': 8.0,
     'L0_tok_Wk': 5.671,
     'L0_attn_time_first': 3.442,
     'L0_ffn_b1': 46.282,
     'L0_ffn_b2': 64.0,
     'L1_attn_Wq': 8.0,
     'L1_attn_Wk': 8.0,
     'L1_attn_Wv': 8.0,
     'L1_attn_Wo': 8.0,
     'L1_ffn_lut': 8.0}
    for name, (base, spread) in spreads.items():
        noise = np.random.default_rng([zlib.crc32(name.encode()), seed]).standard_normal(out[name].shape)
        drawn = base * np.exp(spread * noise) if base else spread * noise
        out[name] = jnp.asarray(drawn.astype(out[name].dtype))
    for name, factor in factors.items():
        out[name] = (out[name] * factor).astype(out[name].dtype)
    return out
```

```python
from contextlib import ExitStack

import concourse.bass as bass
from concourse import mybir

ALU = mybir.AluOpType
ACT = mybir.ActivationFunctionType
AX = mybir.AxisListType
F32 = mybir.dt.float32
F16 = mybir.dt.float16
BF16 = mybir.dt.bfloat16
I32 = mybir.dt.int32
I16 = mybir.dt.int16

P = 128
B, S, D = 8, 256, 512
KT = D // P
NTOK = B * S
NT = NTOK // P
CH = 512
NC = NTOK // CH
TPC = CH // P
LAYERS = 4
HEADS = 16
FF = 2048
GLU = 1376
PW = 2048
EPS = 1e-5
SCALE = float(P) ** -0.5

RG = 2
R_GROUPS = HEADS // RG
F_GROUPS = FF // (4 * P)
M_GROUPS = HEADS // 4
G_TILES = [4, 4, 3]
G_LAST = GLU - 10 * P
G_WIDTH = [KT * t * P for t in G_TILES]
D_WIDTH = [t * D for t in G_TILES]
G_COLS = sum(2 * a + b for a, b in zip(G_WIDTH, D_WIDTH))
WORK = 7430
DEC = 264
DEC_BLOCKS = G_COLS // DEC
DEC_PER_PAIR = DEC_BLOCKS // (R_GROUPS // 2)

P_TOK = 0
P_ABS = P_TOK + LAYERS
P_RW = P_ABS + 2 * F_GROUPS
P_FF = P_RW + 2 * R_GROUPS
P_MO = P_FF + 2 * F_GROUPS
P_GL = P_MO + 4 * M_GROUPS

C_MR, C_MK, C_MV, C_DECAY, C_FIRST, C_B1, C_LUT = 0, 4, 8, 12, 28, 44, 60
N_PAR = 76
K_ID, K_MASK, K_IOTA, K_ROW, K_PET, K_PE = 0, 128, 256, 260, 772, 1796
N_CONST = K_PE + 2 * D

PASSES = ((0, 0), (0, 1), (1, 0))


def build(nc, a):
    with ExitStack() as ctx:
        def sb(name, shape, dt):
            return ctx.enter_context(nc.sbuf_tensor(name, shape, dt))

        def sem(name):
            return ctx.enter_context(nc.semaphore(name))

        h = sb("h", [P, NT, D], F32)
        planes = sb("planes", [P, 6, KT * NTOK], F16)
        wa = sb("wa", [P, 16384], F16)
        stg = sb("stg", [P, 2, PW], F32)
        ident = sb("ident", [P, P], F32)
        identb = sb("identb", [P, P], BF16)
        maskb = sb("maskb", [P, P], BF16)
        par = sb("par", [P, N_PAR], F32)
        mixc = sb("mixc", [P, 12], F32)
        wdec = sb("wdec", [P, HEADS], F32)
        wtmp = sb("wtmp", [P, HEADS], F32)
        cur = sb("cur", [P, 2, 8], F32)
        lutx = sb("lutx", [P, 8], I32)
        stat = sb("stat", [P, 2, 6], F32)
        mv = sb("mv", [P, NT, 2], F32)
        rstd = sb("rstd", [P, NT], F32)
        half = sb("half", [P, TPC], F32)
        wsum = sb("wsum", [P, 8], F32)
        wsc = sb("wsc", [P, 8], F32)
        nmax = sb("nmax", [P, 4], F32)
        rsum = sb("rsum", [P, 4], F32)
        rinv = sb("rinv", [P, 4], F32)
        work = sb("work", [P, WORK], F32)
        ps = ctx.enter_context(nc.psum_tensor("ps", [P, 8, 512], F32))
        dec_dram = a["glu_dec"]

        def w32(at, n):
            return work[:, at:at + n]

        def w16(at, n):
            return work[:, at:at + n // 2].bitcast(F16)

        def act_T(plane):
            return planes[:, plane, :].rearrange("p (k t) -> p k t", k=KT)

        tokT = [act_T(0), act_T(1)]
        encR = [planes[:, 2 + i, :].rearrange("p (t d) -> p t d", t=NT) for i in range(2)]
        setup32 = planes[:, 4:6, :].rearrange("p a b -> p (a b)").bitcast(F32)

        qs = [w16(i * 256, CH) for i in range(2)]
        ks = [w16(512 + i * 256, CH) for i in range(2)]
        prob = w32(1024, 768)
        pT = [w16(1792 + i * 384, 768) for i in range(2)]
        ln_x = [w32(2560 + i * 512, 512) for i in range(2)]
        b2row = w32(3584, 512)
        tok_tmp = [w32(2560 + i * 512, 512) for i in range(2)]

        consts_in, b2_in = sem("consts_in"), sem("b2_in")
        stg_full = [sem(f"stg_full{i}") for i in range(2)]
        setup_done, abs_done, wsum_ps, scale_done = sem("setup_done"), sem("abs_done"), sem("wsum_ps"), sem("scale_done")
        w_ready = sem("w_ready")
        dve_chain, act_chain, pool_chain = sem("dve_chain"), sem("act_chain"), sem("pool_chain")
        dec_chain = sem("dec_chain")
        enc32, enc_hi, enc_lo = sem("enc32"), sem("enc_hi"), sem("enc_lo")
        q_ps, k_ps, q_hi, k_hi, q_split, k_split = (sem(x) for x in ("q_ps", "k_ps", "q_hi", "k_hi", "q_split", "k_split"))
        scored, row_max, exps, inv_sum, probs = (sem(x) for x in ("scored", "row_max", "exps", "inv_sum", "probs"))
        pT_ps, pT_hi, pT_split = sem("pT_ps"), sem("pT_hi"), sem("pT_split")
        to_ps, to_hi, to_free = sem("to_ps"), sem("to_hi"), sem("to_free")
        tow_done = sem("tow_done")
        ln_stat, ln_rstd, ln_x_ready, ln_T, ln_hi, ln_done = (sem(x) for x in ("ln_stat", "ln_rstd", "ln_x_ready", "ln_T", "ln_hi", "ln_done"))
        mix_tmp, mix_y, mix_hi, mix_lo = sem("mix_tmp"), sem("mix_y"), sem("mix_hi"), sem("mix_lo")
        r_ps, k2_ps, v_ps = sem("r_ps"), sem("k2_ps"), sem("v_ps")
        r_sb, k_sb, kv_sb, scan_done, s_sb, o32_sb, o_hi, o_lo = (sem(x) for x in ("r_sb", "k_sb", "kv_sb", "scan_done", "s_sb", "o32_sb", "o_hi", "o_lo"))
        wo_ps, wo_acc = sem("wo_ps"), sem("wo_acc")
        idx_in, dec_out = sem("idx_in"), sem("dec_out")
        par_cur = sem("par_cur")
        h_ps, g32, g_hi, g_lo = sem("h_ps"), sem("g32"), sem("g_hi"), sem("g_lo")
        mv_ps, mv_hi, mv_lo, mo_ps, mo_hi, mo_lo, mw_ps, mw_acc = (sem(x) for x in ("mv_ps", "mv_hi", "mv_lo", "mo_ps", "mo_hi", "mo_lo", "mw_ps", "mw_acc"))
        ga_ps, up_ps, silu_sb, prod_sb, gl_hi, gl_lo = (sem(x) for x in ("ga_ps", "up_ps", "silu_sb", "prod_sb", "gl_hi", "gl_lo"))
        out_sem = sem("out_sem")
        tick = sem("tick")

        te, ve, se, ge = nc.tensor, nc.vector, nc.scalar, nc.gpsimd

        def wait_apart(eng, which, value):
            eng.wait_ge(which, value)
            eng.sem_inc(tick, 1)

        def weight_slot(stage, g):
            if stage == "rwkv":
                return wa[:, (g % 2) * 8192:(g % 2) * 8192 + 8192]
            if stage == "ffn":
                return wa[:, (g % 2) * 8192:(g % 2) * 8192 + 4096]
            b_slot = planes[:, 2:4, :].rearrange("p a b -> p (a b)")
            return b_slot if g % 2 == 0 else wa[:, :]

        def halves(slot, piece, n=PW):
            at = piece * 2 * PW
            return [slot[:, at:at + n], slot[:, at + PW:at + PW + n]]

        def pe_project(u, bank, done, w, x):
            for kt in range(KT):
                for n, (i, j) in enumerate(PASSES):
                    mm = te.matmul(ps[:, bank, :], w(i, kt), x(j, kt), start=(kt == 0 and n == 0),
                                   stop=(kt == KT - 1 and n == 2))
            mm.then_inc(done, 1)

        def pe_scores(pe, u):
            pe.wait_ge(q_split, u + 1)
            pe.wait_ge(k_split, u + 1)
            for b in range(2):
                t0 = b * S
                first = ps[:, 2, b * P:b * P + P]
                second = ps[:, 3, b * S:b * S + S]
                for n, (i, j) in enumerate(PASSES):
                    te.matmul(first, qs[i][:, t0:t0 + P], ks[j][:, t0:t0 + P], start=(n == 0), stop=False)
                te.matmul(first, identb[:, :], maskb[:, :], start=False, stop=True)
                for n, (i, j) in enumerate(PASSES):
                    te.matmul(second, qs[i][:, t0 + P:t0 + S], ks[j][:, t0:t0 + S], start=(n == 0), stop=False)
                mm = te.matmul(second[:, P:S], identb[:, :], maskb[:, :], start=False, stop=True)
            mm.then_inc(scored, 1)

        def pe_transpose_probs(pe, u):
            pe.wait_ge(probs, u + 1)
            for b in range(2):
                for i in range(3):
                    at = b * 384 + i * P
                    mm = te.transpose(ps[:, 4 + b, i * P:i * P + P], prob[:, at:at + P], ident[:, :])
            mm.then_inc(pT_ps, 1)

        def act_q(act, u):
            act.wait_ge(q_ps, u + 1)
            se.activation(qs[0], ps[:, 0, :], ACT.Copy, scale=SCALE).then_inc(q_hi, 1)

        def act_k(act, u):
            act.wait_ge(k_ps, u + 1)
            se.activation(ks[0], ps[:, 1, :], ACT.Copy).then_inc(k_hi, 1)

        def dve_q(dve, u):
            dve.wait_ge(q_hi, u + 1)
            ve.scalar_tensor_tensor(qs[1], ps[:, 0, :], SCALE, qs[0], ALU.mult, ALU.subtract).then_inc(q_split, 1)

        def dve_k(dve, u):
            dve.wait_ge(k_hi, u + 1)
            ve.tensor_tensor(ks[1], ps[:, 1, :], ks[0], ALU.subtract).then_inc(k_split, 1)

        def dve_max(dve, u):
            dve.wait_ge(scored, u + 1)
            ve.tensor_reduce(nmax[:, 0:2], ps[:, 2, 0:S].rearrange("p (b k) -> p b k", b=2), AX.X, ALU.max, negate=True)
            ve.tensor_reduce(nmax[:, 2:4], ps[:, 3, :].rearrange("p (b k) -> p b k", b=2), AX.X, ALU.max, negate=True).then_inc(row_max, 1)

        def act_exp(act, u):
            act.wait_ge(row_max, u + 1)
            for b in range(2):
                se.activation(prob[:, b * 384:b * 384 + P], ps[:, 2, b * P:b * P + P], ACT.Exp,
                              bias=nmax[:, b:b + 1], accum_out=rsum[:, b:b + 1])
                last = se.activation(prob[:, b * 384 + P:b * 384 + 384], ps[:, 3, b * S:b * S + S], ACT.Exp,
                                     bias=nmax[:, 2 + b:3 + b], accum_out=rsum[:, 2 + b:3 + b])
            last.then_inc(exps, 1)

        def dve_norm(dve, u):
            dve.wait_ge(exps, u + 1)
            ve.reciprocal(rinv[:, :], rsum[:, :]).then_inc(inv_sum, 1)
            dve.wait_ge(inv_sum, u + 1)
            for b in range(2):
                x = prob[:, b * 384:b * 384 + P]
                ve.tensor_scalar(x, x, rinv[:, b:b + 1], None, ALU.mult)
                x = prob[:, b * 384 + P:b * 384 + 384]
                last = ve.tensor_scalar(x, x, rinv[:, 2 + b:3 + b], None, ALU.mult)
            last.then_inc(probs, 1)

        pT_view = ps[:, 4:6, 0:384]

        def act_pT(act, u):
            act.wait_ge(pT_ps, u + 1)
            se.activation(pT[0].rearrange("p (b k) -> p b k", b=2), pT_view, ACT.Copy).then_inc(pT_hi, 1)

        def dve_pT(dve, u):
            dve.wait_ge(pT_hi, u + 1)
            ve.tensor_tensor(pT[1].rearrange("p (b k) -> p b k", b=2), pT_view,
                             pT[0].rearrange("p (b k) -> p b k", b=2), ALU.subtract).then_inc(pT_split, 1)

        def tok_project(pe, l, u, c, q, bank, done):
            base = 8192

            def w(i, kt):
                at = base + i * 4096 + q * 512 + kt * P
                if isinstance(l, int):
                    return wa[:, at + l * 1024:at + l * 1024 + P]
                return wa[:, bass.ds(l * 1024 + at, P)]

            pe_project(u, bank, done, w, lambda j, kt: tokT[j][:, kt, c * CH:c * CH + CH])

        TOK_OUT = [("T", i) for i in range(KT)] + [("R", i) for i in (1, 0, 3, 2)]

        def tok_out_mm(pe, u, c, last_layer):
            pe.wait_ge(pT_split, u + 1)
            outs = TOK_OUT[4:] if last_layer else TOK_OUT
            for n, (kind, i) in enumerate(outs):
                bank = 6 + n % 2
                pe.wait_ge(to_free, (96 + 4 * c + n + 1) if last_layer else u * 8 + n + 1)
                if kind == "T":
                    for b in range(2):
                        k0 = c * TPC + 2 * b
                        for m, (x, y) in enumerate(PASSES):
                            te.matmul(ps[:, bank, b * S:b * S + S], encR[x][:, k0, i * P:i * P + P],
                                      pT[y][:, b * 384:b * 384 + S], start=(m == 0), stop=False)
                        for m, (x, y) in enumerate(PASSES):
                            mm = te.matmul(ps[:, bank, b * S + P:b * S + S], encR[x][:, k0 + 1, i * P:i * P + P],
                                           pT[y][:, b * 384 + S:b * 384 + 384], start=False, stop=(m == 2))
                else:
                    b, late = i // 2, i % 2
                    k0 = c * TPC + 2 * b
                    terms = [(k0, P if late else 0)] + ([(k0 + 1, S)] if late else [])
                    for z, (kk, at) in enumerate(terms):
                        for m, (x, y) in enumerate(PASSES):
                            mm = te.matmul(ps[:, bank, :], pT[y][:, b * 384 + at:b * 384 + at + P], encR[x][:, kk, :],
                                           start=(z == 0 and m == 0), stop=(z == len(terms) - 1 and m == 2))
                mm.then_inc(to_ps, 1)

        def tok_dst(c, n, half_):
            kind, i = TOK_OUT[n]
            if kind == "T":
                return tokT[half_][:, i, c * CH:c * CH + CH]
            return encR[half_][:, c * TPC + i, :]

        def ln_dve_chunk(dve, f, c, chain):
            for j in range(TPC):
                tt = c * TPC + j
                chain(ve.bn_stats(stat[:, j % 2, :], h[:, tt, :]))
                chain(ve.bn_aggr(mv[:, tt, :], stat[:, j % 2, :]))
            ve.tensor_scalar(rstd[:, c * TPC:c * TPC + TPC], mv[:, c * TPC:c * TPC + TPC, 1], EPS, None, ALU.add).then_inc(ln_stat, 1)

        def ln_pool_chunk(pool, f, c):
            pool.wait_ge(ln_stat, 4 * f + c + 1)
            r = rstd[:, c * TPC:c * TPC + TPC]
            ge.tensor_tensor(r, r, half[:, :], ALU.pow).then_inc(ln_rstd, 1)

        def ln_dve_x(dve, f, c, j):
            e = 16 * f + 4 * c + j
            tt = c * TPC + j
            if j == 0:
                dve.wait_ge(ln_rstd, 4 * f + c + 1)
            if e >= 2:
                dve.wait_ge(ln_T, e - 1)
            ve.tensor_scalar(ln_x[e % 2], h[:, tt, :], mv[:, tt, 0:1], rstd[:, tt:tt + 1], ALU.subtract,
                             ALU.mult).then_inc(ln_x_ready, 1)

        def ln_pe(pe, f, c, j):
            e = 16 * f + 4 * c + j
            pe.wait_ge(ln_x_ready, e + 1)
            if e >= 2:
                pe.wait_ge(ln_done, e - 1)
            for kt in range(KT):
                mm = te.transpose(ps[:, e % 2, kt * P:kt * P + P], ln_x[e % 2][:, kt * P:kt * P + P], ident[:, :])
            mm.then_inc(ln_T, 1)

        def ln_act(act, f, c, j):
            e = 16 * f + 4 * c + j
            tt = c * TPC + j
            act.wait_ge(ln_T, e + 1)
            src = ps[:, e % 2, :].rearrange("p (k t) -> p k t", k=KT)
            se.activation(tokT[0][:, :, tt * P:tt * P + P], src, ACT.Copy).then_inc(ln_hi, 1)

        def ln_dve_lo(dve, f, c, j):
            e = 16 * f + 4 * c + j
            tt = c * TPC + j
            dve.wait_ge(ln_hi, e + 1 - 16)
            src = ps[:, e % 2, :].rearrange("p (k t) -> p k t", k=KT)
            ve.tensor_tensor(tokT[1][:, :, tt * P:tt * P + P], src, tokT[0][:, :, tt * P:tt * P + P],
                             ALU.subtract).then_inc(ln_done, 1)

        O_RW, O_FF, O_GL = 0, 4 * NC * R_GROUPS, 4 * NC * (R_GROUPS + F_GROUPS)

        def out_tile(pe, n, bank, pairs):
            pe.wait_ge(wo_acc, n + 1)
            for m, (x, y) in enumerate(pairs):
                mm = te.matmul(ps[:, bank, :], x, y, start=(m == 0), stop=(m == len(pairs) - 1))
            mm.then_inc(wo_ps, 1)

        def accumulate(dve, n, bank, tt):
            dve.wait_ge(wo_ps, n + 5)
            ve.tensor_tensor(h[:, tt, :], ps[:, bank, :], h[:, tt, :], ALU.add).then_inc(wo_acc, 1)

        mix = [[act_T(2 * i), act_T(2 * i + 1)] for i in range(3)]
        xT32 = w32(3584, 4 * 514).rearrange("p (k b t) -> p k b t", k=KT, b=2)
        mix_t = [w32(5640 + i * 512, 512) for i in range(2)]
        mix_out = [w32(i * 512, 512) for i in range(2)]
        r_buf, k_buf = w32(0, 512), w32(512, 512)
        kv_buf = w32(1024, 514).rearrange("p (b t) -> p b t", b=2)
        s_buf = w32(1538, 514).rearrange("p (b t) -> p b t", b=2)
        o_buf = w32(2052, 512)
        oT = [[[w16(2564 + ((par_ * 2 + m) * 2 + i) * 256, 512) for i in range(2)] for m in range(RG)] for par_ in range(2)]
        D0 = 2564 + 8 * 256
        dec_idx = w32(D0, DEC).bitcast(I32)
        dec_v = w32(D0 + DEC, 8 * DEC).rearrange("p (j n) -> p j n", j=8)
        dec_m = [work[:, D0 + 9 * DEC + i * DEC // 2:D0 + 9 * DEC + (i + 1) * DEC // 2].bitcast(I16) for i in range(3)]
        assert D0 + 10.5 * DEC <= WORK


        def rw_w(slot, what, i, kt, m):
            at = (what % 2) * 1024 + kt * RG * P + m * P
            return halves(slot, what // 2)[i][:, at:at + P]

        def rw_wo(slot, i, m):
            at = 1024 + m * D
            return halves(slot, 1)[i][:, at:at + D]

        WR_RW = LAYERS
        WR_FF = WR_RW + 2 * R_GROUPS
        WR_MO = WR_FF + 2 * F_GROUPS
        WR_GL = WR_MO + 4 * M_GROUPS
        RW_PAIRS, FF_PAIRS, MO_PAIRS = R_GROUPS // 2, F_GROUPS // 2, M_GROUPS // 2

        def at_most(value, most):
            if isinstance(value, int):
                return value
            return nc.s_assert_within(value, 0, most, skip_runtime_bounds_check_because="the last pair skips the branch")

        class Maybe:

            def __init__(self, eng, cond):
                self.eng, self.cond = eng, cond

            def __enter__(self):
                self.inner = None
                if self.cond is not None:
                    self.inner = self.eng.If(self.cond)
                    self.inner.__enter__()

            def __exit__(self, *e):
                if self.inner is not None:
                    self.inner.__exit__(*e)

        def rw_pe_proj(pe, p, s):
            g, c = s // 4, s % 4
            slot = weight_slot("rwkv", g)
            if c == 0:
                pe.wait_ge(w_ready, p * 4 + WR_RW + 2 * g + 2)
            for m in range(RG):
                n = p * 16 + 2 * s + m
                if not (isinstance(p, int) and s == 0):
                    pe.wait_ge(r_sb, n - 1)
                    pe.wait_ge(k_sb, n - 1)
                    pe.wait_ge(kv_sb, n - 1)
                for what, done in ((0, r_ps), (1, k2_ps), (2, v_ps)):
                    for kt in range(KT):
                        for z, (i, j) in enumerate(PASSES):
                            mm = te.matmul(ps[:, 3 * m + what, :], rw_w(slot, what, i, kt, m),
                                           mix[what][j][:, kt, c * CH:c * CH + CH], start=(kt == 0 and z == 0),
                                           stop=(kt == KT - 1 and z == 2))
                    mm.then_inc(done, 1)

        def rw_pe_out(pe, p, s):
            slot = weight_slot("rwkv", s // 4)
            pe.wait_ge(o_lo, p * 16 + 2 * s + 2)
            for j in range(TPC):
                out_tile(pe, O_RW + p * 32 + 4 * s + j, 6 + j % 2,
                         [(oT[s % 2][m][x][:, j * P:j * P + P], rw_wo(slot, y, m)) for m in range(RG) for x, y in PASSES])

        def rw_act(act, p, s):
            for m in range(RG):
                n = p * 16 + 2 * s + m
                first = isinstance(p, int) and s == 0 and m == 0
                act.wait_ge(r_ps, n + 1)
                if not first:
                    act.wait_ge(o32_sb, n)
                se.activation(r_buf, ps[:, 3 * m, :], ACT.Sigmoid).then_inc(r_sb, 1)
                act.wait_ge(k2_ps, n + 1)
                if not first:
                    act.wait_ge(kv_sb, n)
                se.activation(k_buf, ps[:, 3 * m + 1, :], ACT.Copy).then_inc(k_sb, 1)
                act.wait_ge(o32_sb, n + 1)
                if m == 0 and not (isinstance(p, int) and s < 1):
                    act.wait_ge(wo_ps, O_RW + p * 32 + 4 * s)
                se.activation(oT[s % 2][m][0], o_buf, ACT.Copy).then_inc(o_hi, 1)

        def rw_dve(dve, p, s, m):
            g = s // 4
            if s % 4 == 0 and m == 0:
                col = at_most(p * 4 + 2 * g, HEADS - 2)
                ve.tensor_copy(cur[:, g, 0:2], wdec[:, bass.ds(col, 2)])
                ve.tensor_copy(cur[:, g, 2:4], par[:, bass.ds(col + C_FIRST, 2)]).then_inc(par_cur, 1)
                dve.wait_ge(par_cur, p * 2 + g + 1)
            n = p * 16 + 2 * s + m
            dve.wait_ge(k_sb, n + 1)
            dve.wait_ge(v_ps, n + 1)
            ve.tensor_tensor(kv_buf[:, :, 1:257], k_buf.rearrange("p (b t) -> p b t", b=2),
                             ps[:, 3 * m + 2, :].rearrange("p (b t) -> p b t", b=2), ALU.mult).then_inc(kv_sb, 1)
            dve.wait_ge(kv_sb, n + 1)
            w = cur[:, g, m:m + 1].to_broadcast([P, S])
            for b in range(2):
                ins = ve.tensor_tensor_scan(s_buf[:, b, 1:257], w, kv_buf[:, b, 1:257], 0.0, ALU.mult, ALU.add)
            ins.then_inc(scan_done, 1)
            dve.wait_ge(scan_done, n + 1)
            if not (isinstance(p, int) and s == 0 and m == 0):
                dve.wait_ge(o_lo, n)
                dve.wait_ge(o_hi, n)
            ve.scalar_tensor_tensor(o_buf.rearrange("p (b t) -> p b t", b=2), kv_buf[:, :, 1:257], cur[:, g, 2 + m:3 + m],
                                    s_buf[:, :, 0:256], ALU.mult, ALU.add).then_inc(s_sb, 1)

        def rw_dve_acc(dve, p, s):
            for j in range(TPC):
                accumulate(dve, O_RW + p * 32 + 4 * s + j, 6 + j % 2, (s % 4) * TPC + j)

        def dec_block(dve, p, i):
            k = [0]

            def done(ins, apart=False):
                k[0] += 1
                ins.then_inc(dec_chain, 1)
                value = p * (DEC_PER_PAIR * DEC_OPS) + i * DEC_OPS + k[0] + 1
                if apart:
                    wait_apart(dve, dec_chain, value)
                else:
                    dve.wait_ge(dec_chain, value)

            lut = par[:, C_LUT:C_LUT + 16].bitcast(I32)

            def leaf(j):
                return ve.tensor_scalar(dec_v[:, j, :].bitcast(I32), dec_idx, lutx[:, j:j + 1], lut[:, 2 * j:2 * j + 1],
                                        ALU.bitwise_and, ALU.bitwise_xor)

            dve.wait_ge(dec_chain, p * (DEC_PER_PAIR * DEC_OPS) + i * DEC_OPS + 1)
            dve.wait_ge(idx_in, p * (16 * DEC_PER_PAIR) + 16 * (i + 1))
            done(ve.tensor_copy(dec_m[2], dec_idx))
            ve.tensor_scalar(dec_m[0], dec_m[2], 2, None, ALU.bitwise_and)
            ve.tensor_scalar(dec_m[1], dec_m[2], 4, None, ALU.bitwise_and)
            done(ve.tensor_scalar(dec_idx, dec_idx, 31, 31, ALU.logical_shift_left, ALU.arith_shift_right))
            ve.tensor_scalar(dec_m[2], dec_m[2], 8, None, ALU.bitwise_and)
            for j in range(1, 8):
                leaf(j)
            dve.wait_ge(dec_out, p * (16 * DEC_PER_PAIR) + 16 * (i + 1))
            done(leaf(0), apart=True)
            for b, n in ((0, 4), (1, 2), (2, 1)):
                pairs = dec_v[:, 0:8:8 // (2 * n), :].rearrange("p (n two) c -> p n two c", two=2)
                mask = dec_m[b].rearrange("p (n c) -> p n c", n=1).to_broadcast([P, n, DEC])
                ins = ve.copy_predicated(pairs[:, :, 0, :], mask, pairs[:, :, 1, :])
                if n > 1:
                    done(ins, apart=True)
            k[0] += 1
            assert k[0] == DEC_OPS
            ins.then_inc(dec_chain, 1)

        DEC_OPS = 6

        def rw_pool(pool, p, s):
            for m in range(RG):
                n = p * 16 + 2 * s + m
                pool.wait_ge(s_sb, n + 1)
                pool.wait_ge(r_sb, n + 1)
                ge.tensor_tensor(o_buf, o_buf, r_buf, ALU.mult).then_inc(o32_sb, 1)
                pool.wait_ge(o_hi, n + 1)
                ge.tensor_tensor(oT[s % 2][m][1], o_buf, oT[s % 2][m][0], ALU.subtract).then_inc(o_lo, 1)

        def split(pool, k, before, dst, nth, n=PW):
            wait_apart(pool, stg_full[k], 16 + before * 16)
            ge.tensor_scalar(dst[0], stg[:, k, 0:n], 1.0, 0.0, ALU.mult, ALU.add).then_inc(pool_chain, 1)
            pool.wait_ge(pool_chain, nth + 1)
            ge.tensor_tensor(dst[1], stg[:, k, 0:n], dst[0], ALU.subtract).then_inc(w_ready, 1)

        f32_buf = [w32(i * 512, 512) for i in range(2)]
        gT = [[[w16(1024 + ((q * 4 + m) * 2 + i) * 256, 512) for i in range(2)] for m in range(4)] for q in range(2)]
        magic = 1.5 * 2.0 ** 23

        def ff_pe_proj(pe, p, s):
            g, c = s // 4, s % 4
            slot = weight_slot("ffn", g)
            if c == 0:
                pe.wait_ge(w_ready, p * 4 + WR_FF + 2 * g + 2)
            for m in range(4):
                n = p * 32 + 4 * s + m
                if not (isinstance(p, int) and s == 0):
                    pe.wait_ge(g32, n - 3)
                for kt in range(KT):
                    at = kt * CH + m * P
                    for x in range(2):
                        mm = te.matmul(ps[:, m, :], slot[:, at:at + P], tokT[x][:, kt, c * CH:c * CH + CH],
                                       start=(kt == 0 and x == 0), stop=(kt == KT - 1 and x == 1))
                mm.then_inc(h_ps, 1)

        def ff_pe_out(pe, p, s):
            slot = weight_slot("ffn", s // 4)
            pe.wait_ge(g_lo, p * 32 + 4 * s + 4)
            for j in range(TPC):
                out_tile(pe, O_FF + p * 32 + 4 * s + j, 6 + j % 2,
                         [(gT[s % 2][m][x][:, j * P:j * P + P], slot[:, PW + m * D:PW + m * D + D]) for m in range(4) for x in range(2)])

        def ff_act(act, p, s):
            g = s // 4
            if s % 4 == 0:
                act.wait_ge(par_cur, 2 * RW_PAIRS + p * 2 + g + 1)
            for m in range(4):
                n = p * 32 + 4 * s + m
                first = isinstance(p, int) and s == 0
                act.wait_ge(h_ps, n + 1)
                if not (first and m < 2):
                    act.wait_ge(g_lo, n - 1)
                se.activation(f32_buf[m % 2], ps[:, m, :], ACT.Gelu, bias=cur[:, g, m:m + 1]).then_inc(g32, 1)
                act.wait_ge(g32, n + 1)
                if m == 0 and not (isinstance(p, int) and s < 1):
                    act.wait_ge(wo_ps, O_FF + p * 32 + 4 * s)
                se.activation(gT[s % 2][m][0], f32_buf[m % 2], ACT.Copy).then_inc(g_hi, 1)

        def ff_dve(dve, p, s):
            g = s // 4
            if s % 4 == 0:
                if not (isinstance(p, int) and g == 0):
                    dve.wait_ge(g_hi, p * 32 + 4 * s)
                ve.tensor_copy(cur[:, g, 0:4], par[:, bass.ds(at_most(p * 8 + 4 * g, 12) + C_B1, 4)]).then_inc(par_cur, 1)
            for m in range(4):
                n = p * 32 + 4 * s + m
                dve.wait_ge(g_hi, n + 1)
                ve.tensor_tensor(gT[s % 2][m][1], f32_buf[m % 2], gT[s % 2][m][0], ALU.subtract).then_inc(g_lo, 1)

        def ff_dve_acc(dve, p, s):
            for j in range(TPC):
                accumulate(dve, O_FF + p * 32 + 4 * s + j, 6 + j % 2, (s % 4) * TPC + j)

        def ternary(pool, k, before, which, dst, nth):
            x = stg[:, k, :]
            pool.wait_ge(stg_full[k], 16 + before * 16)
            ge.tensor_scalar(x, x, wsc[:, 4 + which:5 + which], magic, ALU.mult, ALU.add).then_inc(pool_chain, 1)
            pool.wait_ge(pool_chain, nth * 2 + PC_FF + 1)
            ge.tensor_scalar(x, x, -magic, 1.0, ALU.add, ALU.mult).then_inc(pool_chain, 1)
            pool.wait_ge(pool_chain, nth * 2 + PC_FF + 2)
            ge.tensor_scalar(dst, x, 1.0, -1.0, ALU.min, ALU.max).then_inc(w_ready, 1)

        PC_FF = WR_FF
        PC_MO = PC_FF + 4 * F_GROUPS

        MU = LAYERS * NC
        vT = [[planes[:, 4, (q * 2 + i) * 2048:(q * 2 + i) * 2048 + 2048].rearrange("p (t d) -> p t d", t=TPC) for i in range(2)] for q in range(2)]
        oH = [[[planes[:, 5, ((q * 4 + j) * 2 + i) * 512:((q * 4 + j) * 2 + i) * 512 + 512] for i in range(2)] for j in range(4)] for q in range(2)]
        VB, OB, FB = 7, 6, 7

        def mo_u(p, s, j):
            return p * 32 + MU + 4 * s + j

        def mo_q(pe, p, s, j, which):
            g, c = s // 4, s % 4
            slot = weight_slot("moba", g)
            u = mo_u(p, s, j)
            pe_project(u, which, k_ps if which else q_ps,
                       lambda i, kt: halves(slot, which)[i][:, kt * CH + j * P:kt * CH + j * P + P],
                       lambda i, kt: tokT[i][:, kt, c * CH:c * CH + CH])

        def mo_v(pe, p, s, j):
            g, c = s // 4, s % 4
            slot = weight_slot("moba", g)
            if c == 0 and j == 0:
                pe.wait_ge(w_ready, p * 8 + WR_MO + 4 * g + 4)
            pe.wait_ge(mv_lo, p * 32 + 4 * s + j)
            if not (isinstance(p, int) and s == 0):
                pe.wait_ge(mw_acc, p * 32 + 4 * s + MV_ACC[j])
            tt = c * TPC + j
            for kt in range(KT):
                for z, (x, y) in enumerate(PASSES):
                    mm = te.matmul(ps[:, VB, :], tokT[x][:, kt, tt * P:tt * P + P], halves(slot, 2)[y][:, kt * CH:kt * CH + CH],
                                   start=(kt == 0 and z == 0), stop=(kt == KT - 1 and z == 2))
            mm.then_inc(mv_ps, 1)

        OUT_AT = [[], [0], [1], [2, 3]]
        MV_ACC = [0, 0, 1, 2]

        def mo_out(pe, p, s, tt, prev_slot):
            pe.wait_ge(mo_lo, p * 32 + 4 * s)
            pe.wait_ge(mw_acc, p * 32 + 4 * s + tt + 4)
            q = (s - 1) % 2
            pairs = [(oH[q][j][x][:, tt * P:tt * P + P], halves(prev_slot, 3)[y][:, j * D:j * D + D]) for j in range(4) for x, y in PASSES]
            for z, (x, y) in enumerate(pairs):
                mm = te.matmul(ps[:, FB, :], x, y, start=(z == 0), stop=(z == len(pairs) - 1))
            mm.then_inc(mw_ps, 1)

        def mo_pv(pe, p, s, j):
            u = mo_u(p, s, j)
            pe.wait_ge(pT_split, u + 1)
            for b in range(2):
                for z, (x, y) in enumerate(PASSES):
                    te.matmul(ps[:, OB, b * S:b * S + S], vT[s % 2][x][:, 2 * b, j * P:j * P + P], pT[y][:, b * 384:b * 384 + S],
                              start=(z == 0), stop=False)
                for z, (x, y) in enumerate(PASSES):
                    mm = te.matmul(ps[:, OB, b * S + P:b * S + S], vT[s % 2][x][:, 2 * b + 1, j * P:j * P + P],
                                   pT[y][:, b * 384 + S:b * 384 + 384], start=False, stop=(z == 2))
            mm.then_inc(mo_ps, 1)

        def mo_rounds(eng, body):
            with eng.Fori(0, MO_PAIRS) as p:
                for s in range(8):
                    nstep = (p, s + 1) if s < 7 else (p + 1, 0)
                    cond = None if s < 7 else p < MO_PAIRS - 1
                    for j in range(4):
                        nround = (p, s, j + 1) if j < 3 else (*nstep, 0)
                        body(p, s, j, nround, nstep, cond if j == 3 else None, cond)

        def mo_pe(pe, p, s, j, nround, nstep, rcond, scond):
            u = mo_u(p, s, j)
            with Maybe(pe, rcond):
                mo_q(pe, *nround, 0)
            with Maybe(pe, scond):
                mo_v(pe, *nstep, j)
            with Maybe(pe, rcond):
                mo_q(pe, *nround, 1)
            pe_transpose_probs(pe, u)
            with Maybe(pe, (p > 0) if s == 0 and OUT_AT[j] else None):
                for tt in OUT_AT[j]:
                    if tt < 3:
                        if s < 7:
                            pe.wait_ge(mv_lo, p * 32 + 4 * (s + 1) + j + 1)
                        else:
                            with Maybe(pe, scond):
                                pe.wait_ge(mv_lo, p * 32 + 4 * (s + 1) + j + 1)
                    mo_out(pe, p, s, tt, weight_slot("moba", ((s - 1) % 8) // 4))
            with Maybe(pe, rcond):
                pe_scores(pe, mo_u(*nround))
            mo_pv(pe, p, s, j)

        def mo_act_v(act, p, s, j):
            n = p * 32 + 4 * s + j
            act.wait_ge(mv_ps, n + 1)
            se.activation(vT[s % 2][0][:, j, :], ps[:, VB, :], ACT.Copy).then_inc(mv_hi, 1)

        def mo_act(act, p, s, j, nround, nstep, rcond, scond):
            u = mo_u(p, s, j)
            with Maybe(act, rcond):
                act_q(act, mo_u(*nround))
            with Maybe(act, scond):
                mo_act_v(act, *nstep, j)
            with Maybe(act, rcond):
                act_k(act, mo_u(*nround))
            act_pT(act, u)
            with Maybe(act, rcond):
                act_exp(act, mo_u(*nround))
            n = p * 32 + 4 * s + j
            act.wait_ge(mo_ps, n + 1)
            se.activation(oH[s % 2][j][0], ps[:, OB, :], ACT.Copy).then_inc(mo_hi, 1)

        def mo_dve_v(dve, p, s, j):
            n = p * 32 + 4 * s + j
            dve.wait_ge(mv_hi, n + 1)
            ve.tensor_tensor(vT[s % 2][1][:, j, :], ps[:, VB, :], vT[s % 2][0][:, j, :], ALU.subtract).then_inc(mv_lo, 1)

        def mo_dve_acc(dve, p, s, tt):
            dve.wait_ge(mw_ps, p * 32 + 4 * s + tt + 5)
            x = h[:, ((s - 1) % 4) * TPC + tt, :]
            ve.tensor_tensor(x, ps[:, FB, :], x, ALU.add).then_inc(mw_acc, 1)

        def mo_dve(dve, p, s, j, nround, nstep, rcond, scond):
            u = mo_u(p, s, j)
            with Maybe(dve, rcond):
                dve_q(dve, mo_u(*nround))
            with Maybe(dve, scond):
                mo_dve_v(dve, *nstep, j)
            with Maybe(dve, rcond):
                dve_k(dve, mo_u(*nround))
            dve_pT(dve, u)
            with Maybe(dve, (p > 0) if s == 0 and OUT_AT[j] else None):
                for tt in OUT_AT[j]:
                    mo_dve_acc(dve, p, s, tt)
            with Maybe(dve, rcond):
                dve_max(dve, mo_u(*nround))
                dve_norm(dve, mo_u(*nround))
            n = p * 32 + 4 * s + j
            dve.wait_ge(mo_hi, n + 1)
            ve.tensor_tensor(oH[s % 2][j][1], ps[:, OB, :], oH[s % 2][j][0], ALU.subtract).then_inc(mo_lo, 1)

        GL_T = [(g, c) for g in range(3) for c in range(NC)]

        def gl_base(t):
            return sum(G_TILES[g] for g, _ in GL_T[:t])

        sg_buf = [w32(i * 512, 512) for i in range(2)]
        hT = [[[w16(1024 + ((q * 4 + m) * 2 + i) * 256, 512) for i in range(2)] for m in range(4)] for q in range(2)]

        def gl_rows(g, m):
            return G_LAST if g == 2 and m == 2 else P

        def gl_pe_proj(pe, t):
            g, c = GL_T[t]
            slot = weight_slot("glu", g)
            if c == 0:
                pe.wait_ge(w_ready, WR_GL + 3 * g + 3)
            for m in range(G_TILES[g]):
                n = gl_base(t) + m
                if n >= 2:
                    pe.wait_ge(prod_sb, n - 1)
                W = G_TILES[g] * P
                for piece, done in ((0, ga_ps), (1, up_ps)):
                    bank = 2 * (n % 2) + piece
                    for kt in range(KT):
                        for z, (i, j) in enumerate(PASSES):
                            at = kt * W + m * P
                            mm = te.matmul(ps[:, bank, :], halves(slot, piece)[i][:, at:at + P],
                                           tokT[j][:, kt, c * CH:c * CH + CH], start=(kt == 0 and z == 0),
                                           stop=(kt == KT - 1 and z == 2))
                    mm.then_inc(done, 1)

        def gl_pe_out(pe, t):
            g, c = GL_T[t]
            slot = weight_slot("glu", g)
            pe.wait_ge(gl_lo, gl_base(t + 1))
            for j in range(TPC):
                pairs = []
                for m in range(G_TILES[g]):
                    r = gl_rows(g, m)
                    pairs += [(hT[t % 2][m][x][0:r, j * P:j * P + P], halves(slot, 2)[y][0:r, m * D:m * D + D]) for x, y in PASSES]
                out_tile(pe, O_GL + 4 * t + j, 6 + j % 2, pairs)

        def gl_act(act, t):
            g, c = GL_T[t]
            for m in range(G_TILES[g]):
                n = gl_base(t) + m
                act.wait_ge(ga_ps, n + 1)
                if n >= 2:
                    act.wait_ge(gl_lo, n - 1)
                se.activation(sg_buf[n % 2], ps[:, 2 * (n % 2), :], ACT.Silu).then_inc(silu_sb, 1)
                act.wait_ge(prod_sb, n + 1)
                if m == 0 and t >= 2:
                    act.wait_ge(wo_ps, O_GL + 4 * t)
                se.activation(hT[t % 2][m][0], sg_buf[n % 2], ACT.Copy).then_inc(gl_hi, 1)

        def gl_dve(dve, t):
            g, c = GL_T[t]
            for m in range(G_TILES[g]):
                n = gl_base(t) + m
                dve.wait_ge(silu_sb, n + 1)
                dve.wait_ge(up_ps, n + 1)
                ve.tensor_tensor(sg_buf[n % 2], sg_buf[n % 2], ps[:, 2 * (n % 2) + 1, :], ALU.mult).then_inc(prod_sb, 1)
                dve.wait_ge(gl_hi, n + 1)
                ve.tensor_tensor(hT[t % 2][m][1], sg_buf[n % 2], hT[t % 2][m][0], ALU.subtract).then_inc(gl_lo, 1)

        def mix_act_copy(act, c, j):
            e = 4 * c + j
            act.wait_ge(ln_T, e + 1)
            if e >= 0 and c == 0 and j == 0:
                act.wait_ge(setup_done, 2)
            if c > 0 and j == 0:
                act.wait_ge(mix_y, 12 * c)
            b, at = j // 2, 1 + (j % 2) * P
            src = ps[:, e % 2, :].rearrange("p (k t) -> p k t", k=KT)
            se.activation(xT32[:, :, b, at:at + P], src, ACT.Copy).then_inc(ln_done, 1)

        def mix_ops(c):
            return [(12 * c + 3 * kt + w, kt, w) for kt in range(KT) for w in range(3)]

        def mix_pool(pool, c):
            for e, kt, w in mix_ops(c):
                if e % 12 == 0:
                    pool.wait_ge(ln_done, 4 * c + 4)
                if e >= 2:
                    pool.wait_ge(mix_y, e - 1)
                col = (0, 4, 8)[w] + kt
                ge.tensor_scalar(mix_t[e % 2].rearrange("p (b t) -> p b t", b=2), xT32[:, kt, :, 0:256],
                                 mixc[:, col:col + 1], 0.0, ALU.mult, ALU.add).then_inc(mix_tmp, 1)

        def mix_dve(dve, c):
            for e, kt, w in mix_ops(c):
                dve.wait_ge(mix_tmp, e + 1)
                if e >= 2:
                    dve.wait_ge(mix_lo, e - 1)
                col = (C_MR, C_MK, C_MV)[w] + kt
                ve.scalar_tensor_tensor(mix_out[e % 2].rearrange("p (b t) -> p b t", b=2), xT32[:, kt, :, 1:257],
                                        par[:, col:col + 1], mix_t[e % 2].rearrange("p (b t) -> p b t", b=2),
                                        ALU.mult, ALU.add).then_inc(mix_y, 1)
                if e % 12 > 0:
                    mix_dve_lo(dve, e - 1)

        def mix_dst(e, i):
            c, r = e // 12, e % 12
            return mix[r % 3][i][:, r // 3, c * CH:c * CH + CH]

        def mix_dve_lo(dve, e):
            dve.wait_ge(mix_hi, e + 1)
            ve.tensor_tensor(mix_dst(e, 1), mix_out[e % 2], mix_dst(e, 0), ALU.subtract).then_inc(mix_lo, 1)

        def mix_act(act, c):
            for e, kt, w in mix_ops(c):
                act.wait_ge(mix_y, e + 1)
                se.activation(mix_dst(e, 0), mix_out[e % 2], ACT.Copy).then_inc(mix_hi, 1)

        TOK_HALF = 4

        def tok_pe(pe, l, c, nxt):
            u = l * 4 + c
            if nxt is not None:
                tok_project(pe, nxt[0], u + 1, nxt[1], 0, 0, q_ps)
                tok_project(pe, nxt[0], u + 1, nxt[1], 1, 1, k_ps)
            pe_transpose_probs(pe, u)
            if nxt is not None:
                pe_scores(pe, u + 1)
            tok_out_mm(pe, u, c, isinstance(l, int) and l == LAYERS - 1)

        def tok_act(act, l, c, nxt):
            u = l * 4 + c
            last = isinstance(l, int) and l == LAYERS - 1
            if nxt is not None:
                act_q(act, u + 1)
                act_k(act, u + 1)
            act_pT(act, u)

            def out(n):
                act.wait_ge(to_ps, u * 8 + n + 1)
                se.activation(tok_dst(c, n, 0), ps[:, 6 + n % 2, :], ACT.Copy).then_inc(to_hi, 1)

            if not last:
                out(0), out(1)
            if nxt is not None:
                act_exp(act, u + 1)
            if not last:
                for n in range(2, 8):
                    out(n)
            if c % 2:
                k = c // 2
                act.wait_ge(stg_full[k], l * 16 + 16 * (P_ABS // 2 + 1))
                se.activation(stg[:, k, :], stg[:, k, :], ACT.Abs, accum_out=wabs(l, k)).then_inc(abs_done, 1)

        def wabs(l, k):
            return wsum[:, k * 4 + l:k * 4 + l + 1] if isinstance(l, int) else wsum[:, bass.ds(l + k * 4, 1)]

        def tok_dve(dve, l, c, nxt):
            u = l * 4 + c
            last = isinstance(l, int) and l == LAYERS - 1
            if nxt is not None:
                dve_q(dve, u + 1)
                dve_k(dve, u + 1)
            dve_pT(dve, u)
            if nxt is not None:
                dve_max(dve, u + 1)

            def out(n):
                if last:
                    i = TOK_OUT[4 + n][1]
                    dve.wait_ge(to_ps, 96 + 4 * c + n + 1)
                    ve.tensor_copy(h[:, c * TPC + i, :], ps[:, 6 + n % 2, :]).then_inc(to_free, 1)
                else:
                    dve.wait_ge(to_hi, u * 8 + n + 1)
                    ve.tensor_tensor(tok_dst(c, n, 1), ps[:, 6 + n % 2, :], tok_dst(c, n, 0), ALU.subtract).then_inc(to_free, 1)

            n_out = 4 if last else 8
            for n in range(n_out // 2):
                out(n)
            if nxt is not None:
                dve_norm(dve, u + 1)
            for n in range(n_out // 2, n_out):
                out(n)

        def tower(eng, body):
            with eng.Fori(0, LAYERS - 1) as l:
                for c in range(NC):
                    body(eng, l, c, (l, c + 1) if c < NC - 1 else (l + 1, 0))
            for c in range(NC):
                body(eng, LAYERS - 1, c, (LAYERS - 1, c + 1) if c < NC - 1 else None)

        def steps8(eng, pairs, own, nxt):
            with eng.Fori(0, pairs) as p:
                for s in range(8):
                    if s < 7:
                        nxt(eng, p, s + 1)
                    else:
                        with eng.If(p < pairs - 1):
                            nxt(eng, p + 1, 0)
                    own(eng, p, s)

        row = setup32[:, 0:D]
        peT = setup32[:, D:D + KT * S].rearrange("p (k t) -> p k t", k=KT)
        pe_rows = setup32[:, D + KT * S:D + KT * S + 2 * D].rearrange("p (a d) -> p a d", a=2)
        tok_cols = setup32[:, 2560:2560 + NTOK].bitcast(I32)
        tok_rows_i = setup32[:, 4608:4624].bitcast(I32)
        tok_rows = setup32[:, 4624:4640]
        ones = setup32[:, 4640:4768]
        mask32 = work[:, 6000:6132]
        iota = work[:, 6128:6132]

        def enc_dst(e, half_):
            c, n = e // 8, e % 8
            return tokT[half_][:, n, c * CH:c * CH + CH] if n < 4 else encR[half_][:, c * TPC + n - 4, :]

        block = ctx.enter_context(nc.Block())

        @block.sync
        def _(sp):
            sp.dma_start(mask32, a["consts"][:, P:P + 132]).then_inc(consts_in, 16)
            sp.dma_start(setup32[:, 0:2560], a["consts"][:, K_ROW:K_ROW + 2560]).then_inc(consts_in, 16)
            sp.dma_start(tok_cols, a["tok_cols"]).then_inc(consts_in, 16)
            sp.dma_start(tok_rows_i, a["tok_rows"]).then_inc(consts_in, 16)
            sp.dma_start(ident[:, :], a["consts"][:, 0:P]).then_inc(consts_in, 16)
            sp.dma_start(par[:, :], a["par"]).then_inc(consts_in, 16)
            for i in range(LAYERS):
                if i >= 2:
                    sp.wait_ge(w_ready, i - 1)
                sp.dma_start(stg[:, i % 2, 0:1024], a["tok_w"][i]).then_inc(stg_full[i % 2], 16)
            for i in range(2 * F_GROUPS):
                if i < 2:
                    sp.wait_ge(w_ready, LAYERS - 1 + i)
                else:
                    sp.wait_ge(abs_done, i - 1)
                sp.dma_start(stg[:, i % 2, :], a["ff_w"][i]).then_inc(stg_full[i % 2], 16)
            for i in range(4):
                if i < 2:
                    sp.wait_ge(abs_done, 2 * F_GROUPS - 1 + i)
                else:
                    sp.wait_ge(w_ready, WR_RW + i - 1)
                sp.dma_start(stg[:, i % 2, :], a["rw_w"][i]).then_inc(stg_full[i % 2], 16)
            sp.wait_ge(mix_lo, 12 * NC)
            sp.dma_start(dec_idx, a["glu_idx"][:, 0:DEC]).then_inc(idx_in, 16)
            with sp.Fori(0, RW_PAIRS) as p:
                def rw_piece(k):
                    with sp.If(p < RW_PAIRS - 1):
                        wait_apart(sp, w_ready, p * 4 + WR_RW + 4 + k - 1)
                        sp.dma_start(stg[:, k % 2, :], a["rw_w"][bass.ds(at_most(p * 4 + 4 + k, 2 * R_GROUPS - 1), 1)].rearrange("a p n -> (a p) n")).then_inc(stg_full[k % 2], 16)

                def dec_done(i, k):
                    wait_apart(sp, dec_chain, p * (DEC_PER_PAIR * DEC_OPS) + i * DEC_OPS + k + 1)

                def load_idx(pp, i):
                    sp.dma_start(dec_idx, a["glu_idx"][:, bass.ds(at_most(pp * (DEC_PER_PAIR * DEC) + i * DEC, G_COLS - DEC), DEC)]).then_inc(idx_in, 16)

                for i in range(DEC_PER_PAIR):
                    dec_done(i, 3)
                    if i < DEC_PER_PAIR - 1:
                        load_idx(p, i + 1)
                    else:
                        with sp.If(p < RW_PAIRS - 1):
                            load_idx(p + 1, 0)
                    dec_done(i, DEC_OPS)
                    sp.dma_start(dec_dram[:, bass.ds(p * (DEC_PER_PAIR * DEC) + i * DEC, DEC)], dec_v[:, 0, :]).then_inc(dec_out, 16)
                    if i in (3, 5, 11, 13):
                        rw_piece((3, 5, 11, 13).index(i))
            sp.wait_ge(dec_chain, DEC_BLOCKS * DEC_OPS + 1)
            sp.wait_ge(wo_ps, O_FF + 4)
            sp.dma_start(b2row, a["b2"]).then_inc(b2_in, 16)
            with sp.Fori(0, F_GROUPS) as q:
                for k in range(2):
                    wait_apart(sp, w_ready, q * 2 + WR_FF + k - 1)
                    sp.dma_start(stg[:, k, :], a["ff_w"][bass.ds(q * 2 + k, 1)].rearrange("a p n -> (a p) n")).then_inc(stg_full[k], 16)
            with sp.Fori(0, 2 * M_GROUPS) as q:
                for k in range(2):
                    wait_apart(sp, w_ready, q * 2 + WR_MO + k - 1)
                    sp.dma_start(stg[:, k, :], a["mo_w"][bass.ds(q * 2 + k, 1)].rearrange("a p n -> (a p) n")).then_inc(stg_full[k], 16)
            sp.wait_ge(dec_out, 16 * DEC_BLOCKS + 16)
            at = 0
            for i in range(9):
                n = (G_WIDTH if i % 3 < 2 else D_WIDTH)[i // 3]
                sp.wait_ge(w_ready, WR_GL + i - 1)
                sp.dma_start(stg[:, i % 2, 0:n], dec_dram[:, at:at + n]).then_inc(stg_full[i % 2], 16)
                at += n
            for c in range(NC):
                sp.wait_ge(wo_acc, 2 + O_GL + 4 * (2 * NC + c) + 4)
                sp.dma_start(a["out"][:, c * TPC:c * TPC + TPC, :], h[:, c * TPC:c * TPC + TPC, :]).then_inc(out_sem, 16)
            sp.wait_ge(out_sem, 16 * NC)

        @block.gpsimd
        def _(pool):
            for i in range(LAYERS):
                split(pool, i % 2, i // 2, [wa[:, 8192 + x * 4096 + i * 1024:8192 + x * 4096 + i * 1024 + 1024] for x in range(2)], i, 1024)

            def rw_split(g, pp, k):
                slot = weight_slot("rwkv", g)
                idx = pp * 4 + 2 * (g % 2) + k if not isinstance(pp, int) else 4 * pp + 2 * (g % 2) + k
                before = P_RW // 2 + pp * 2 + (g % 2) if isinstance(pp, int) else pp * 2 + (P_RW // 2 + g % 2)
                split(pool, k, before, halves(slot, k), WR_RW + idx if isinstance(pp, int) else idx + WR_RW)

            rw_split(0, 0, 0), rw_split(0, 0, 1)
            pool.wait_ge(q_ps, MU)
            pool.wait_ge(k_ps, MU)
            rw_split(1, 0, 0), rw_split(1, 0, 1)
            for c in range(NC):
                ln_pool_chunk(pool, 0, c)
            for c in range(NC):
                mix_pool(pool, c)
            with pool.Fori(0, RW_PAIRS) as p:
                for s in range(8):
                    rw_pool(pool, p, s)
                    if s in (1, 2):
                        with pool.If(p > 0):
                            pool.wait_ge(wo_ps, p * 32 + 4)
                            rw_split(1, p, s - 1)
                    if s in (5, 6):
                        with pool.If(p < RW_PAIRS - 1):
                            pool.wait_ge(wo_ps, p * 32 + 20)
                            rw_split(0, p + 1, s - 5)

            def ffn_w(g):
                for k in range(2):
                    dst = weight_slot("ffn", g)[:, k * PW:k * PW + PW]
                    ternary(pool, k, P_FF // 2 + g, k, dst, 2 * g + k)

            def mo_w(g):
                for k in range(4):
                    split(pool, k % 2, P_MO // 2 + 2 * g + k // 2, halves(weight_slot("moba", g), k), PC_MO + 4 * g + k)

            pool.wait_ge(scale_done, 1)
            ffn_w(0)
            pool.wait_ge(wo_ps, O_FF + 4)
            ffn_w(1)
            for c in range(NC):
                ln_pool_chunk(pool, 1, c)
            for g in (2, 3):
                pool.wait_ge(wo_ps, O_FF + 4 + 16 * (g - 1))
                ffn_w(g)
            mo_w(0)
            for c in range(NC):
                ln_pool_chunk(pool, 2, c)
            mo_w(1)
            for g in (2, 3):
                pool.wait_ge(mw_ps, 8 + 16 * (g - 1))
                mo_w(g)

            def gl_w(g):
                for k in range(3):
                    i = 3 * g + k
                    n = (G_WIDTH if k < 2 else D_WIDTH)[g]
                    split(pool, i % 2, (P_GL + i) // 2, halves(weight_slot("glu", g), k, n), PC_MO + 16 + i, n)

            pool.wait_ge(mw_ps, 8 + 48)
            gl_w(0)
            for c in range(NC):
                ln_pool_chunk(pool, 3, c)
            gl_w(1)
            pool.wait_ge(wo_ps, O_GL + 20)
            gl_w(2)

        @block.scalar
        def _(act):
            def enc(e):
                act.wait_ge(enc32, e + 1)
                se.activation(enc_dst(e, 0), tok_tmp[e % 2], ACT.Copy).then_inc(enc_hi, 1)

            for e in range(32):
                enc(e)
            act_q(act, 0)
            act_k(act, 0)
            act_exp(act, 0)
            tower(act, tok_act)
            act.wait_ge(setup_done, 1)
            se.activation(wtmp[:, :], par[:, C_DECAY:C_DECAY + HEADS], ACT.Exp).then_inc(act_chain, 1)
            act.wait_ge(act_chain, 1)
            se.activation(wdec[:, :], wtmp[:, :], ACT.Exp, scale=-1.0).then_inc(act_chain, 1)
            for c in range(NC):
                for j in range(TPC):
                    mix_act_copy(act, c, j)
                mix_act(act, c)
            rw_act(act, 0, 0)
            with act.Fori(0, RW_PAIRS) as p:
                for s in range(8):
                    if s < 7:
                        rw_act(act, p, s + 1)
                    else:
                        with act.If(p < RW_PAIRS - 1):
                            rw_act(act, p + 1, 0)
            for c in range(NC):
                for j in range(TPC):
                    ln_act(act, 1, c, j)
            ff_act(act, 0, 0)
            with act.Fori(0, FF_PAIRS) as p:
                for s in range(8):
                    if s < 7:
                        ff_act(act, p, s + 1)
                    else:
                        with act.If(p < FF_PAIRS - 1):
                            ff_act(act, p + 1, 0)
            for c in range(NC):
                for j in range(TPC):
                    ln_act(act, 2, c, j)
            for j in range(TPC):
                mo_act_v(act, 0, 0, j)
            act_q(act, MU)
            act_k(act, MU)
            act_exp(act, MU)
            mo_rounds(act, lambda *x: mo_act(act, *x))
            for c in range(NC):
                for j in range(TPC):
                    ln_act(act, 3, c, j)
            for t in range(len(GL_T)):
                gl_act(act, t)

        @block.vector
        def _(dve):
            k = [0]

            def chain(ins):
                k[0] += 1
                ins.then_inc(dve_chain, 1)
                dve.wait_ge(dve_chain, k[0])

            ve.memset(ones, 1.0).then_inc(to_free, 2)
            ve.memset(wsum[:, :], 0.0).then_inc(wo_ps, 4)
            ve.memset(half[:, :], -0.5).then_inc(wo_acc, 2)
            ve.memset(rsum[:, :], 0.0).then_inc(dec_out, 16)
            ve.memset(stat[:, :, :], 0.0).then_inc(dec_chain, 1)
            ve.memset(mv[:, :, :], 0.0).then_inc(mw_ps, 8)
            ve.memset(rstd[:, :], 0.0).then_inc(mw_acc, 8)
            dve.wait_ge(consts_in, 96)
            lut = par[:, C_LUT:C_LUT + 16].bitcast(I32).rearrange("p (j b) -> p j b", b=2)
            ve.tensor_tensor(lutx[:, :], lut[:, :, 0], lut[:, :, 1], ALU.bitwise_xor)
            ve.tensor_copy(identb[:, :], ident[:, :])
            ve.tensor_copy(maskb[:, :], mask32[:, 0:P])
            ve.tensor_scalar(mixc[:, :], par[:, 0:12], -1.0, 1.0, ALU.mult, ALU.add).then_inc(setup_done, 1)
            chain(ve.tensor_copy(tok_rows, tok_rows_i))

            def enc_low(e):
                dve.wait_ge(enc_hi, e + 1)
                ve.tensor_tensor(enc_dst(e, 1), tok_tmp[e % 2], enc_dst(e, 0), ALU.subtract).then_inc(enc_lo, 1)

            for e in range(32):
                c, n = e // 8, e % 8
                if e >= 2:
                    dve.wait_ge(enc_lo, e - 1)
                if n < 4:
                    for b in range(2):
                        ins = ve.scalar_tensor_tensor(tok_tmp[e % 2][:, b * S:b * S + S], tok_cols[:, c * CH + b * S:c * CH + b * S + S],
                                                      iota[:, n:n + 1], peT[:, n, :], ALU.is_equal, ALU.add)
                else:
                    tt = c * TPC + n - 4
                    ins = ve.scalar_tensor_tensor(tok_tmp[e % 2], row, tok_rows[:, tt:tt + 1], pe_rows[:, tt % 2, :],
                                                  ALU.is_equal, ALU.add)
                ins.then_inc(enc32, 1)
                if e > 0:
                    enc_low(e - 1)
            enc_low(31)
            dve_q(dve, 0)
            dve_k(dve, 0)
            dve_max(dve, 0)
            dve_norm(dve, 0)
            tower(dve, tok_dve)
            dve.wait_ge(wsum_ps, 1)
            chain(ve.tensor_reduce(wsc[:, 0:2], ps[:, 6, 0:8].rearrange("p (w g) -> p w g", w=2), AX.X, ALU.add))
            chain(ve.tensor_scalar(wsc[:, 2:4], wsc[:, 0:2], 1.0 / (FF * D), 1e-8, ALU.mult, ALU.max))
            ve.reciprocal(wsc[:, 4:6], wsc[:, 2:4]).then_inc(scale_done, 1)
            ve.memset(xT32[:, :, :, 0:1], 0.0).then_inc(setup_done, 1)
            for c in range(NC):
                ln_dve_chunk(dve, 0, c, chain)
            for c in range(NC):
                for j in range(TPC):
                    ln_dve_x(dve, 0, c, j)
                mix_dve(dve, c)
                mix_dve_lo(dve, 12 * c + 11)
            for b in range(2):
                for x in (kv_buf, s_buf):
                    ins = ve.memset(x[:, b, 0:1], 0.0)
            dve.wait_ge(act_chain, 2)
            for m in range(RG):
                rw_dve(dve, 0, 0, m)
            with dve.Fori(0, RW_PAIRS) as p:
                for s in range(8):
                    for m in range(RG):
                        if s < 7:
                            rw_dve(dve, p, s + 1, m)
                        else:
                            with dve.If(p < RW_PAIRS - 1):
                                rw_dve(dve, p + 1, 0, m)
                        if m == 0:
                            dec_block(dve, p, 2 * s)
                    rw_dve_acc(dve, p, s)
                    dec_block(dve, p, 2 * s + 1)

            def ln_phase(f):
                for c in range(NC):
                    ln_dve_chunk(dve, f, c, chain)
                for c in range(NC):
                    for j in range(TPC):
                        ln_dve_x(dve, f, c, j)
                        if (c, j) > (0, 0):
                            ln_dve_lo(dve, f, (4 * c + j - 1) // 4, (4 * c + j - 1) % 4)
                ln_dve_lo(dve, f, NC - 1, TPC - 1)

            ln_phase(1)
            dve.wait_ge(ln_x_ready, 32)
            dve.wait_ge(b2_in, 16)
            for tt in range(NT):
                ins = ve.tensor_tensor(h[:, tt, :], h[:, tt, :], b2row, ALU.add)
            chain(ins)
            ff_dve(dve, 0, 0)
            with dve.Fori(0, FF_PAIRS) as p:
                for s in range(8):
                    if s < 7:
                        ff_dve(dve, p, s + 1)
                    else:
                        with dve.If(p < FF_PAIRS - 1):
                            ff_dve(dve, p + 1, 0)
                    ff_dve_acc(dve, p, s)
            ln_phase(2)
            for j in range(TPC):
                mo_dve_v(dve, 0, 0, j)
            dve_q(dve, MU)
            dve_k(dve, MU)
            dve_max(dve, MU)
            dve_norm(dve, MU)
            mo_rounds(dve, lambda *x: mo_dve(dve, *x))
            for tt in range(TPC):
                mo_dve_acc(dve, MO_PAIRS, 0, tt)
            ln_phase(3)
            for t in range(len(GL_T)):
                gl_dve(dve, t)
                if t > 0:
                    for j in range(TPC):
                        accumulate(dve, O_GL + 4 * (t - 1) + j, 6 + j % 2, GL_T[t - 1][1] * TPC + j)
            for j in range(TPC):
                accumulate(dve, O_GL + 44 + j, 6 + j % 2, 12 + j)

        @block.tensor
        def _(pe):
            pe.wait_ge(enc_lo, 32)
            pe.wait_ge(w_ready, LAYERS)
            tok_project(pe, 0, 0, 0, 0, 0, q_ps)
            tok_project(pe, 0, 0, 0, 1, 1, k_ps)
            pe_scores(pe, 0)
            tower(pe, tok_pe)
            pe.wait_ge(abs_done, 2 * F_GROUPS)
            pe.wait_ge(to_free, 2 + 96 + 16)
            te.matmul(ps[:, 6, 0:8], ones, wsum[:, :], start=True, stop=True).then_inc(wsum_ps, 1)
            for c in range(NC):
                for j in range(TPC):
                    ln_pe(pe, 0, c, j)
            pe.wait_ge(mix_lo, 48)
            pe.wait_ge(ln_done, 16)
            rw_pe_proj(pe, 0, 0)
            steps8(pe, RW_PAIRS, rw_pe_out, rw_pe_proj)
            for c in range(NC):
                for j in range(TPC):
                    ln_pe(pe, 1, c, j)
            pe.wait_ge(ln_done, 32)
            ff_pe_proj(pe, 0, 0)
            steps8(pe, FF_PAIRS, ff_pe_out, ff_pe_proj)
            for c in range(NC):
                for j in range(TPC):
                    ln_pe(pe, 2, c, j)
            pe.wait_ge(ln_done, 48)
            for j in range(TPC):
                mo_v(pe, 0, 0, j)
            mo_q(pe, 0, 0, 0, 0)
            mo_q(pe, 0, 0, 0, 1)
            pe_scores(pe, MU)
            mo_rounds(pe, lambda *x: mo_pe(pe, *x))
            for tt in range(TPC):
                mo_out(pe, MO_PAIRS, 0, tt, weight_slot("moba", 1))
            for c in range(NC):
                for j in range(TPC):
                    ln_pe(pe, 3, c, j)
            pe.wait_ge(ln_done, 64)
            gl_pe_proj(pe, 0)
            for t in range(len(GL_T)):
                if t < len(GL_T) - 1:
                    gl_pe_proj(pe, t + 1)
                gl_pe_out(pe, t)


def kernel(**inputs):
    import numpy as np
    import concourse.bacc as bacc
    from concourse.bass_utils import run_bass_kernel_spmd

    x = np.asarray(inputs["x"])
    W = {k: np.asarray(v) for k, v in inputs.items()}

    def rows(w, n):
        return w.reshape(-1, P, n).transpose(1, 0, 2)

    def flat(*parts):
        return np.concatenate([p.reshape(P, -1) for p in parts], axis=1)

    def pad(w, n, axis):
        out = np.zeros([n if i == axis else s for i, s in enumerate(w.shape)], w.dtype)
        out[(slice(None),) * axis + (slice(0, w.shape[axis]),)] = w
        return out

    tok_w = np.stack([flat(rows(W["L0_tok_Wq"][i], P), rows(W["L0_tok_Wk"][i], P)) for i in range(LAYERS)])
    r, k, v = (W["L0_attn_" + n].T for n in ("Wr", "Wk", "Wv"))
    o = W["L0_attn_Wo"].T
    n = RG * P
    rw_w = np.stack([q for g in range(R_GROUPS) for q in (
        flat(rows(r[:, g * n:g * n + n], n), rows(k[:, g * n:g * n + n], n)),
        flat(rows(v[:, g * n:g * n + n], n), rows(o[g * n:g * n + n], D)))])
    w1, w2 = W["L0_ffn_w1"].T, W["L0_ffn_w2"].T
    ff_w = np.stack([q for g in range(F_GROUPS) for q in (
        flat(rows(w1[:, g * CH:g * CH + CH], CH)), flat(rows(w2[g * CH:g * CH + CH], D)))])
    mq, mk, mvv, mo = (W["L1_attn_" + n] for n in ("Wq", "Wk", "Wv", "Wo"))
    mo_w = np.stack([q for g in range(M_GROUPS) for q in (
        *(flat(rows(w[:, g * CH:g * CH + CH], CH)) for w in (mq, mk, mvv)), flat(rows(mo[g * CH:g * CH + CH], D)))])
    full = sum(G_TILES) * P
    gi, ui = (pad(W[n].T, full, 1) for n in ("L1_ffn_gate_idx", "L1_ffn_up_idx"))
    di = pad(W["L1_ffn_down_idx"].T, full, 0)
    parts, at = [], 0
    for t in G_TILES:
        parts += [rows(gi[:, at:at + t * P], t * P), rows(ui[:, at:at + t * P], t * P), rows(di[at:at + t * P], D)]
        at += t * P
    glu_idx = flat(*parts)

    def cols(w):
        return w.reshape(-1, P).T

    par = flat(cols(W["L0_attn_time_mix_r"]), cols(W["L0_attn_time_mix_k"]), cols(W["L0_attn_time_mix_v"]),
               cols(W["L0_attn_time_decay"]), cols(W["L0_attn_time_first"]), cols(W["L0_ffn_b1"]),
               np.broadcast_to(W["L1_ffn_lut"], (P, 16)))

    f = np.float32
    pos = np.arange(S, dtype=f)[:, None]
    div = np.exp(-(np.log(f(10000.0)) / f(D)) * np.arange(0, D, 2, dtype=f))
    enc = np.zeros((S, D), f)
    enc[:, 0::2] = np.sin(pos * div)
    enc[:, 1::2] = np.cos(pos * div)
    i = np.arange(P)
    consts = np.concatenate([
        np.eye(P, dtype=f), np.where(i[None, :] > i[:, None], f(-1e30), f(0)),
        (i[:, None] + P * np.arange(KT)[None, :]).astype(f),
        np.broadcast_to(np.arange(D, dtype=f), (P, D)), flat(rows(enc.T, S)), flat(rows(enc, D))], axis=1)

    arrays = {
        "tok_cols": np.broadcast_to(x.reshape(1, NTOK), (P, NTOK)), "tok_rows": x.reshape(NT, P).T, "consts": consts, "par": par,
        "b2": np.broadcast_to(W["L0_ffn_b2"], (P, D)), "tok_w": tok_w, "rw_w": rw_w, "ff_w": ff_w, "mo_w": mo_w, "glu_idx": glu_idx,
    }
    arrays = {name: np.ascontiguousarray(v) for name, v in arrays.items()}
    nc = bacc.Bacc("TRN2", target_bir_lowering=False, num_devices=1)
    a = {name: nc.dram_tensor("in_" + name, v.shape, mybir.dt.from_np(v.dtype), kind="ExternalInput").ap() for name, v in arrays.items()}
    a["glu_dec"] = nc.dram_tensor("glu_dec", (P, G_COLS), F32, kind="Internal").ap()
    out = nc.dram_tensor("out", (B, S, D), F32, kind="ExternalOutput").ap()
    a["out"] = out.rearrange("b s d -> (b s) d").rearrange("(t p) d -> p t d", p=P)
    build(nc, a)
    got = run_bass_kernel_spmd(nc, [{"in_" + name: v for name, v in arrays.items()}], core_ids=[0])
    return got.results[0]["out"]
```

```python
from contextlib import ExitStack

import concourse.bass as bass
from concourse import mybir

ALU = mybir.AluOpType
ACT = mybir.ActivationFunctionType
AX = mybir.AxisListType
F32 = mybir.dt.float32
F16 = mybir.dt.float16
BF16 = mybir.dt.bfloat16
I32 = mybir.dt.int32
I16 = mybir.dt.int16

P = 128
B, S, D = 8, 256, 512
KT = D // P
NTOK = B * S
NT = NTOK // P
CH = 512
NC = NTOK // CH
TPC = CH // P
LAYERS = 4
HEADS = 16
FF = 2048
GLU = 1376
PW = 2048
EPS = 1e-5
SCALE = float(P) ** -0.5

RG = 2
R_GROUPS = HEADS // RG
F_GROUPS = FF // (4 * P)
M_GROUPS = HEADS // 4
G_TILES = [4, 4, 3]
G_LAST = GLU - 10 * P
G_WIDTH = [KT * t * P for t in G_TILES]
D_WIDTH = [t * D for t in G_TILES]
G_COLS = sum(2 * a + b for a, b in zip(G_WIDTH, D_WIDTH))
WORK = 7430
DEC = 264
DEC_BLOCKS = G_COLS // DEC
DEC_PER_PAIR = DEC_BLOCKS // (R_GROUPS // 2)

P_TOK = 0
P_ABS = P_TOK + LAYERS
P_RW = P_ABS + 2 * F_GROUPS
P_FF = P_RW + 2 * R_GROUPS
P_MO = P_FF + 2 * F_GROUPS
P_GL = P_MO + 4 * M_GROUPS

C_MR, C_MK, C_MV, C_DECAY, C_FIRST, C_B1, C_LUT = 0, 4, 8, 12, 28, 44, 60
N_PAR = 76
K_ID, K_MASK, K_IOTA, K_ROW, K_PET, K_PE = 0, 128, 256, 260, 772, 1796
N_CONST = K_PE + 2 * D

PASSES = ((0, 0), (0, 1), (1, 0))


def build(nc, a):
    with ExitStack() as ctx:
        def sb(name, shape, dt):
            return ctx.enter_context(nc.sbuf_tensor(name, shape, dt))

        def sem(name):
            return ctx.enter_context(nc.semaphore(name))

        h = sb("h", [P, NT, D], F32)
        planes = sb("planes", [P, 6, KT * NTOK], F16)
        wa = sb("wa", [P, 16384], F16)
        stg = sb("stg", [P, 2, PW], F32)
        ident = sb("ident", [P, P], F32)
        identb = sb("identb", [P, P], BF16)
        maskb = sb("maskb", [P, P], BF16)
        par = sb("par", [P, N_PAR], F32)
        mixc = sb("mixc", [P, 12], F32)
        wdec = sb("wdec", [P, HEADS], F32)
        wtmp = sb("wtmp", [P, HEADS], F32)
        cur = sb("cur", [P, 2, 8], F32)
        lutx = sb("lutx", [P, 8], I32)
        stat = sb("stat", [P, TPC, 6], F32)
        mv = sb("mv", [P, NT, 2], F32)
        rstd = sb("rstd", [P, NT], F32)
        half = sb("half", [P, TPC], F32)
        wsum = sb("wsum", [P, 8], F32)
        wsc = sb("wsc", [P, 8], F32)
        nmax = sb("nmax", [P, 4], F32)
        rsum = sb("rsum", [P, 4], F32)
        rinv = sb("rinv", [P, 4], F32)
        work = sb("work", [P, WORK], F32)
        ps = ctx.enter_context(nc.psum_tensor("ps", [P, 8, 512], F32))
        dec_dram = a["glu_dec"]

        def w32(at, n):
            return work[:, at:at + n]

        def w16(at, n):
            return work[:, at:at + n // 2].bitcast(F16)

        def act_T(plane):
            return planes[:, plane, :].rearrange("p (k t) -> p k t", k=KT)

        tokT = [act_T(0), act_T(1)]

        def encR(half_, tt):
            at = (tt % TPC) * NTOK + (tt // TPC) * CH
            return planes[:, 2 + half_, at:at + D]

        setup32 = planes[:, 4:6, :].rearrange("p a b -> p (a b)").bitcast(F32)

        qs = [w16(i * 256, CH) for i in range(2)]
        ks = [w16(512 + i * 256, CH) for i in range(2)]
        prob = w32(1024, 768)
        pT = [w16(1792 + i * 384, 768) for i in range(2)]
        b2row = w32(5382, 512)
        tok_tmp = [w32(2560 + i * 512, 512) for i in range(4)]

        stg_full = [sem(f"stg_full{i}") for i in range(2)]
        consts_in, rest_in, b2_in = (sem(x) for x in (
            "consts_in", "rest_in", "b2_in"))
        w_ready = sem("w_ready")
        setup_done, abs_done, wsum_ps, scale_done, b2_added = (sem(x) for x in (
            "setup_done", "abs_done", "wsum_ps", "scale_done", "b2_added"))
        dve_chain, act_chain, pool_chain, dec_chain = (sem(x) for x in (
            "dve_chain", "act_chain", "pool_chain", "dec_chain"))
        enc32, enc_hi, enc_lo, enc_lo_rows = (sem(x) for x in (
            "enc32", "enc_hi", "enc_lo", "enc_lo_rows"))
        q_ps, k_ps, q_hi, k_hi, q_split, k_split = (sem(x) for x in (
            "q_ps", "k_ps", "q_hi", "k_hi", "q_split", "k_split"))
        scored, row_max, exps, inv_sum, probs = (sem(x) for x in (
            "scored", "row_max", "exps", "inv_sum", "probs"))
        pT_ps, pT_hi, pT_split = (sem(x) for x in (
            "pT_ps", "pT_hi", "pT_split"))
        to_ps, to_hi, to_free = (sem(x) for x in (
            "to_ps", "to_hi", "to_free"))
        ln_stat, ln_rstd, ln_x_ready, ln_T, ln_hi, ln_done = (sem(x) for x in (
            "ln_stat", "ln_rstd", "ln_x_ready", "ln_T", "ln_hi", "ln_done"))
        mix_tmp, mix_y, mix_hi, mix_lo, mix_lo_v = (sem(x) for x in (
            "mix_tmp", "mix_y", "mix_hi", "mix_lo", "mix_lo_v"))
        r_ps, k2_ps, v_ps = (sem(x) for x in (
            "r_ps", "k2_ps", "v_ps"))
        r_sb, k_sb, kv_sb, scan_done, s_sb, o32_sb, o_hi, o_lo = (sem(x) for x in (
            "r_sb", "k_sb", "kv_sb", "scan_done", "s_sb", "o32_sb", "o_hi", "o_lo"))
        wo_ps, wo_acc = (sem(x) for x in (
            "wo_ps", "wo_acc"))
        idx_in, dec_out = (sem(x) for x in (
            "idx_in", "dec_out"))
        par_cur = sem("par_cur")
        h_ps, g32, g_hi, g_lo = (sem(x) for x in (
            "h_ps", "g32", "g_hi", "g_lo"))
        mv_ps, mv_hi, mv_lo, mo_ps, mo_hi, mo_lo, mw_ps, mw_acc = (sem(x) for x in (
            "mv_ps", "mv_hi", "mv_lo", "mo_ps", "mo_hi", "mo_lo", "mw_ps", "mw_acc"))
        ga_ps, up_ps, silu_sb, prod_sb, gl_hi, gl_lo = (sem(x) for x in (
            "ga_ps", "up_ps", "silu_sb", "prod_sb", "gl_hi", "gl_lo"))
        out_sem, tick = (sem(x) for x in (
            "out_sem", "tick"))

        te, ve, se, ge = nc.tensor, nc.vector, nc.scalar, nc.gpsimd

        def wait_apart(eng, which, value):
            eng.wait_ge(which, value)
            eng.sem_inc(tick, 1)

        def weight_slot(stage, g):
            if stage == "rwkv":
                return wa[:, (g % 2) * 8192:(g % 2) * 8192 + 8192]
            if stage == "ffn":
                return wa[:, (g % 2) * 8192:(g % 2) * 8192 + 4096]
            b_slot = planes[:, 2:4, :].rearrange("p a b -> p (a b)")
            return b_slot if g % 2 == 0 else wa[:, :]

        def halves(slot, piece, n=PW):
            at = piece * 2 * PW
            return [slot[:, at:at + n], slot[:, at + PW:at + PW + n]]

        def pe_project(u, bank, done, w, x, between=None):
            for kt in range(KT):
                if kt == 1 and between is not None:
                    between()
                for n, (i, j) in enumerate(PASSES):
                    mm = te.matmul(ps[:, bank, :], w(i, kt), x(j, kt), start=(kt == 0 and n == 0),
                                   stop=(kt == KT - 1 and n == 2))
            mm.then_inc(done, 1)

        def pe_scores(pe, u):
            pe.wait_ge(q_split, u + 1)
            pe.wait_ge(k_split, u + 1)
            for b in range(2):
                t0 = b * S
                first = ps[:, 2, b * P:b * P + P]
                second = ps[:, 3, b * S:b * S + S]
                for n, (i, j) in enumerate(PASSES):
                    te.matmul(first, qs[i][:, t0:t0 + P], ks[j][:, t0:t0 + P], start=(n == 0), stop=False)
                te.matmul(first, identb[:, :], maskb[:, :], start=False, stop=True)
                for n, (i, j) in enumerate(PASSES):
                    te.matmul(second, qs[i][:, t0 + P:t0 + S], ks[j][:, t0:t0 + S], start=(n == 0), stop=False)
                mm = te.matmul(second[:, P:S], identb[:, :], maskb[:, :], start=False, stop=True)
            mm.then_inc(scored, 1)

        def pe_transpose_probs(pe, u):
            pe.wait_ge(probs, u + 1)
            for b in range(2):
                for i in range(3):
                    at = b * 384 + i * P
                    mm = te.transpose(ps[:, 4 + b, i * P:i * P + P], prob[:, at:at + P], ident[:, :])
            mm.then_inc(pT_ps, 1)

        def act_q(act, u):
            act.wait_ge(q_ps, u + 1)
            se.activation(qs[0], ps[:, 0, :], ACT.Copy, scale=SCALE).then_inc(q_hi, 1)

        def act_k(act, u):
            act.wait_ge(k_ps, u + 1)
            se.activation(ks[0], ps[:, 1, :], ACT.Copy).then_inc(k_hi, 1)

        def dve_q(dve, u):
            dve.wait_ge(q_hi, u + 1)
            ve.scalar_tensor_tensor(qs[1], ps[:, 0, :], SCALE, qs[0], ALU.mult, ALU.subtract).then_inc(q_split, 1)

        def dve_k(dve, u):
            dve.wait_ge(k_hi, u + 1)
            ve.tensor_tensor(ks[1], ps[:, 1, :], ks[0], ALU.subtract).then_inc(k_split, 1)

        def dve_max(dve, u):
            dve.wait_ge(scored, u + 1)
            ve.tensor_reduce(nmax[:, 0:2], ps[:, 2, 0:S].rearrange("p (b k) -> p b k", b=2), AX.X, ALU.max, negate=True)
            ve.tensor_reduce(nmax[:, 2:4], ps[:, 3, :].rearrange("p (b k) -> p b k", b=2), AX.X, ALU.max, negate=True).then_inc(row_max, 1)

        def act_exp(act, u):
            act.wait_ge(row_max, u + 1)
            for b in range(2):
                se.activation(prob[:, b * 384:b * 384 + P], ps[:, 2, b * P:b * P + P], ACT.Exp,
                              bias=nmax[:, b:b + 1], accum_out=rsum[:, b:b + 1])
                last = se.activation(prob[:, b * 384 + P:b * 384 + 384], ps[:, 3, b * S:b * S + S], ACT.Exp,
                                     bias=nmax[:, 2 + b:3 + b], accum_out=rsum[:, 2 + b:3 + b])
            last.then_inc(exps, 1)

        def dve_norm(dve, u):
            dve.wait_ge(exps, u + 1)
            ve.reciprocal(rinv[:, :], rsum[:, :]).then_inc(inv_sum, 1)
            dve.wait_ge(inv_sum, u + 1)
            for b in range(2):
                x = prob[:, b * 384:b * 384 + P]
                ve.tensor_scalar(x, x, rinv[:, b:b + 1], None, ALU.mult)
                x = prob[:, b * 384 + P:b * 384 + 384]
                last = ve.tensor_scalar(x, x, rinv[:, 2 + b:3 + b], None, ALU.mult)
            last.then_inc(probs, 1)

        pT_view = ps[:, 4:6, 0:384]

        def act_pT(act, u):
            act.wait_ge(pT_ps, u + 1)
            se.activation(pT[0].rearrange("p (b k) -> p b k", b=2), pT_view, ACT.Copy).then_inc(pT_hi, 1)

        def dve_pT(dve, u):
            dve.wait_ge(pT_hi, u + 1)
            ve.tensor_tensor(pT[1].rearrange("p (b k) -> p b k", b=2), pT_view,
                             pT[0].rearrange("p (b k) -> p b k", b=2), ALU.subtract).then_inc(pT_split, 1)

        def tok_project(pe, l, u, c, q, bank, done):
            if q == 0:
                pe.wait_ge(enc_lo, 4 * (c + 1))
                if c == 0:
                    pe.wait_ge(w_ready, l + 1)
            base = 8192

            def w(i, kt):
                at = base + i * 4096 + q * 512 + kt * P
                if isinstance(l, int):
                    return wa[:, at + l * 1024:at + l * 1024 + P]
                return wa[:, bass.ds(l * 1024 + at, P)]

            pe_project(u, bank, done, w, lambda j, kt: tokT[j][:, kt, c * CH:c * CH + CH])

        TOK_OUT = [("T", i) for i in range(KT)] + [("R", i) for i in (1, 0, 3, 2)]

        TOK_BANK = [0, 1, 6, 7] * 2

        def tok_out_mm(pe, u, c, last_layer):
            pe.wait_ge(pT_split, u + 1)
            pe.wait_ge(enc_lo_rows, 4 * (c + 1))
            outs = TOK_OUT[4:] if last_layer else TOK_OUT
            for n, (kind, i) in enumerate(outs):
                bank = TOK_BANK[n]
                pe.wait_ge(to_free, (96 + 4 * c + n + 1) if last_layer else u * 8 + n + 1)
                if kind == "T":
                    for b in range(2):
                        k0 = c * TPC + 2 * b
                        for m, (x, y) in enumerate(PASSES):
                            te.matmul(ps[:, bank, b * S:b * S + S], encR(x, k0)[:, i * P:i * P + P],
                                      pT[y][:, b * 384:b * 384 + S], start=(m == 0), stop=False)
                        for m, (x, y) in enumerate(PASSES):
                            mm = te.matmul(ps[:, bank, b * S + P:b * S + S], encR(x, k0 + 1)[:, i * P:i * P + P],
                                           pT[y][:, b * 384 + S:b * 384 + 384], start=False, stop=(m == 2))
                else:
                    b, late = i // 2, i % 2
                    k0 = c * TPC + 2 * b
                    terms = [(k0, P if late else 0)] + ([(k0 + 1, S)] if late else [])
                    for z, (kk, at) in enumerate(terms):
                        for m, (x, y) in enumerate(PASSES):
                            mm = te.matmul(ps[:, bank, :], pT[y][:, b * 384 + at:b * 384 + at + P], encR(x, kk),
                                           start=(z == 0 and m == 0), stop=(z == len(terms) - 1 and m == 2))
                mm.then_inc(to_ps, 1)

        def tok_dst(c, n, half_):
            kind, i = TOK_OUT[n]
            if kind == "T":
                return tokT[half_][:, i, c * CH:c * CH + CH]
            return encR(half_, c * TPC + i)

        def ln_x(e):
            if e < 32:
                x = planes[:, 4 + e % 4 // 2, :].bitcast(F32).rearrange("p (k t) -> p k t", k=KT)
                at = ((NC - 1) * CH if e < 16 else 0) // 2
                return x[:, 2 * (e % 2):2 * (e % 2) + 2, at:at + CH // 2]
            return w32(5382 + e % 4 * 512, 512).rearrange("p (k t) -> p k t", k=2)

        def ln_bank(e):
            return ps[:, (6 if e < 16 else 4) + e % 2, :]

        def ln_dve_chunk(dve, f, c, chain):
            for j in range(TPC):
                ins = ve.bn_stats(stat[:, j, :], h[:, c * TPC + j, :])
            chain(ins)
            for j in range(TPC):
                ins = ve.bn_aggr(mv[:, c * TPC + j, :], stat[:, j, :])
            chain(ins)
            ve.tensor_scalar(rstd[:, c * TPC:c * TPC + TPC], mv[:, c * TPC:c * TPC + TPC, 1], EPS, None, ALU.add).then_inc(ln_stat, 1)

        def ln_pool_chunk(pool, f, c):
            pool.wait_ge(ln_stat, 4 * f + c + 1)
            r = rstd[:, c * TPC:c * TPC + TPC]
            ge.tensor_tensor(r, r, half[:, :], ALU.pow).then_inc(ln_rstd, 1)

        def ln_dve_x(dve, f, c, j):
            e = 16 * f + 4 * c + j
            tt = c * TPC + j
            if j == 0:
                dve.wait_ge(ln_rstd, 4 * f + c + 1)
            if e >= 4:
                dve.wait_ge(ln_T, e - 3)
            ve.tensor_scalar(ln_x(e), h[:, tt, :].rearrange("p (k t) -> p k t", k=2), mv[:, tt, 0:1], rstd[:, tt:tt + 1], ALU.subtract,
                             ALU.mult).then_inc(ln_x_ready, 1)

        def ln_pe(pe, f, c, j):
            e = 16 * f + 4 * c + j
            pe.wait_ge(ln_x_ready, e + 1)
            if e >= 2:
                pe.wait_ge(ln_done, e - 1)
            for kt in range(KT):
                mm = te.transpose(ln_bank(e)[:, kt * P:kt * P + P], ln_x(e)[:, kt // 2, kt % 2 * P:kt % 2 * P + P], ident[:, :])
            mm.then_inc(ln_T, 1)

        def ln_act(act, f, c, j):
            e = 16 * f + 4 * c + j
            tt = c * TPC + j
            act.wait_ge(ln_T, e + 1)
            src = ln_bank(e).rearrange("p (k t) -> p k t", k=KT)
            se.activation(tokT[0][:, :, tt * P:tt * P + P], src, ACT.Copy).then_inc(ln_hi, 1)

        def ln_dve_lo(dve, f, c, j):
            e = 16 * f + 4 * c + j
            tt = c * TPC + j
            dve.wait_ge(ln_hi, e + 1 - 16)
            src = ln_bank(e).rearrange("p (k t) -> p k t", k=KT)
            ve.tensor_tensor(tokT[1][:, :, tt * P:tt * P + P], src, tokT[0][:, :, tt * P:tt * P + P],
                             ALU.subtract).then_inc(ln_done, 1)

        def ln_chunk(eng, part, f, c):
            for j in range(TPC):
                part(eng, f, c, j)

        def last_pair(eng, p, pairs):
            return eng.If(p > pairs - 2)

        def first_pair(eng, p):
            return eng.If(p < 1)

        O_RW, O_FF, O_GL = 0, 4 * NC * R_GROUPS, 4 * NC * (R_GROUPS + F_GROUPS)

        def out_tile(pe, n, bank, pairs):
            pe.wait_ge(wo_acc, n + 1)
            for m, (x, y) in enumerate(pairs):
                mm = te.matmul(ps[:, bank, :], x, y, start=(m == 0), stop=(m == len(pairs) - 1))
            mm.then_inc(wo_ps, 1)

        def accumulate(dve, n, bank, tt):
            dve.wait_ge(wo_ps, n + 5)
            ve.tensor_tensor(h[:, tt, :], ps[:, bank, :], h[:, tt, :], ALU.add).then_inc(wo_acc, 1)

        mix = [[act_T(2 * i), act_T(2 * i + 1)] for i in range(3)]
        xT32 = w32(3584, 4 * 514).rearrange("p (k b t) -> p k b t", k=KT, b=2)
        mix_t = [w32(5640 + i * 512, 512) for i in range(2)]
        mix_out = [w32(at, 512) for at in (2560, 3072, 6664)]
        r_buf, k_buf = w32(0, 512), w32(512, 512)
        kv_buf = w32(1024, 514).rearrange("p (b t) -> p b t", b=2)
        s_buf = w32(1538, 514).rearrange("p (b t) -> p b t", b=2)
        o_buf = w32(2052, 512)
        oT = [[[w16(2564 + ((par_ * 2 + m) * 2 + i) * 256, 512) for i in range(2)] for m in range(RG)] for par_ in range(2)]
        D0 = 2564 + 8 * 256
        dec_idx = w32(D0, DEC).bitcast(I32)
        dec_v = w32(D0 + DEC, 8 * DEC).rearrange("p (j n) -> p j n", j=8)
        dec_m = [work[:, D0 + 9 * DEC + i * DEC // 2:D0 + 9 * DEC + (i + 1) * DEC // 2].bitcast(I16) for i in range(3)]
        assert D0 + 10.5 * DEC <= WORK


        def rw_w(slot, what, i, kt, m):
            at = (what % 2) * 1024 + kt * RG * P + m * P
            return halves(slot, what // 2)[i][:, at:at + P]

        def rw_wo(slot, i, m):
            at = 1024 + m * D
            return halves(slot, 1)[i][:, at:at + D]

        WR_RW = LAYERS
        WR_FF = WR_RW + 2 * R_GROUPS
        WR_MO = WR_FF + 2 * F_GROUPS
        WR_GL = WR_MO + 4 * M_GROUPS
        RW_PAIRS, FF_PAIRS, MO_PAIRS = R_GROUPS // 2, F_GROUPS // 2, M_GROUPS // 2

        def at_most(value, most):
            if isinstance(value, int):
                return value
            return nc.s_assert_within(value, 0, most, skip_runtime_bounds_check_because="the last pair skips the branch")

        class Maybe:

            def __init__(self, eng, cond):
                self.eng, self.cond = eng, cond

            def __enter__(self):
                self.inner = None
                if self.cond is not None:
                    self.inner = self.eng.If(self.cond)
                    self.inner.__enter__()

            def __exit__(self, *e):
                if self.inner is not None:
                    self.inner.__exit__(*e)

        def rw_pe_proj(pe, p, s, m):
            g, c = s // 4, s % 4
            slot = weight_slot("rwkv", g)
            if c == 0 and m == 0:
                pe.wait_ge(w_ready, p * 4 + WR_RW + 2 * g + 2)
            n = p * 16 + 2 * s + m
            if not (isinstance(p, int) and s == 0):
                pe.wait_ge(r_sb, n - 1)
                pe.wait_ge(k_sb, n - 1)
                pe.wait_ge(kv_sb, n - 1)
            for what, done in ((0, r_ps), (1, k2_ps), (2, v_ps)):
                for kt in range(KT):
                    for z, (i, j) in enumerate(PASSES):
                        mm = te.matmul(ps[:, 3 * m + what, :], rw_w(slot, what, i, kt, m),
                                       mix[what][j][:, kt, c * CH:c * CH + CH], start=(kt == 0 and z == 0),
                                       stop=(kt == KT - 1 and z == 2))
                mm.then_inc(done, 1)

        def rw_pe_out(pe, p, s, m):
            slot = weight_slot("rwkv", s // 4)
            pe.wait_ge(o_lo, p * 16 + 2 * s + 2)
            for j in (2 * m, 2 * m + 1):
                out_tile(pe, O_RW + p * 32 + 4 * s + j, 6 + j % 2,
                         [(oT[s % 2][k][x][:, j * P:j * P + P], rw_wo(slot, y, k)) for k in range(RG) for x, y in PASSES])

        def rw_act(act, p, s):
            for m in range(RG):
                n = p * 16 + 2 * s + m
                first = isinstance(p, int) and s == 0 and m == 0
                act.wait_ge(r_ps, n + 1)
                if not first:
                    act.wait_ge(o32_sb, n)
                se.activation(r_buf, ps[:, 3 * m, :], ACT.Sigmoid).then_inc(r_sb, 1)
                act.wait_ge(k2_ps, n + 1)
                if not first:
                    act.wait_ge(kv_sb, n)
                se.activation(k_buf, ps[:, 3 * m + 1, :], ACT.Copy).then_inc(k_sb, 1)
                act.wait_ge(o32_sb, n + 1)
                if m == 0 and not (isinstance(p, int) and s < 1):
                    act.wait_ge(wo_ps, O_RW + p * 32 + 4 * s)
                se.activation(oT[s % 2][m][0], o_buf, ACT.Copy).then_inc(o_hi, 1)

        def rw_dve(dve, p, s, m):
            g = s // 4
            if s % 4 == 0 and m == 0:
                col = at_most(p * 4 + 2 * g, HEADS - 2)
                ve.tensor_copy(cur[:, g, 0:2], wdec[:, bass.ds(col, 2)])
                ve.tensor_copy(cur[:, g, 2:4], par[:, bass.ds(col + C_FIRST, 2)]).then_inc(par_cur, 1)
                dve.wait_ge(par_cur, p * 2 + g + 1)
            n = p * 16 + 2 * s + m
            dve.wait_ge(k_sb, n + 1)
            dve.wait_ge(v_ps, n + 1)
            ve.tensor_tensor(kv_buf[:, :, 1:257], k_buf.rearrange("p (b t) -> p b t", b=2),
                             ps[:, 3 * m + 2, :].rearrange("p (b t) -> p b t", b=2), ALU.mult).then_inc(kv_sb, 1)
            dve.wait_ge(kv_sb, n + 1)
            w = cur[:, g, m:m + 1].to_broadcast([P, S])
            for b in range(2):
                ins = ve.tensor_tensor_scan(s_buf[:, b, 1:257], w, kv_buf[:, b, 1:257], 0.0, ALU.mult, ALU.add)
            ins.then_inc(scan_done, 1)
            dve.wait_ge(scan_done, n + 1)
            if not (isinstance(p, int) and s == 0 and m == 0):
                dve.wait_ge(o_lo, n)
                dve.wait_ge(o_hi, n)
            ve.scalar_tensor_tensor(o_buf.rearrange("p (b t) -> p b t", b=2), kv_buf[:, :, 1:257], cur[:, g, 2 + m:3 + m],
                                    s_buf[:, :, 0:256], ALU.mult, ALU.add).then_inc(s_sb, 1)

        def rw_dve_acc(dve, p, s, m):
            for j in (2 * m, 2 * m + 1):
                accumulate(dve, O_RW + p * 32 + 4 * s + j, 6 + j % 2, (s % 4) * TPC + j)

        def dec_block(dve, p, i):
            k = [0]

            def done(ins, apart=False):
                k[0] += 1
                ins.then_inc(dec_chain, 1)
                value = p * (DEC_PER_PAIR * DEC_OPS) + i * DEC_OPS + k[0] + 1
                if apart:
                    wait_apart(dve, dec_chain, value)
                else:
                    dve.wait_ge(dec_chain, value)

            lut = par[:, C_LUT:C_LUT + 16].bitcast(I32)

            def leaf(j):
                return ve.tensor_scalar(dec_v[:, j, :].bitcast(I32), dec_idx, lutx[:, j:j + 1], lut[:, 2 * j:2 * j + 1],
                                        ALU.bitwise_and, ALU.bitwise_xor)

            dve.wait_ge(dec_chain, p * (DEC_PER_PAIR * DEC_OPS) + i * DEC_OPS + 1)
            dve.wait_ge(idx_in, p * (16 * DEC_PER_PAIR) + 16 * (i + 1))
            done(ve.tensor_copy(dec_m[2], dec_idx))
            ve.tensor_scalar(dec_m[0], dec_m[2], 2, None, ALU.bitwise_and)
            ve.tensor_scalar(dec_m[1], dec_m[2], 4, None, ALU.bitwise_and)
            done(ve.tensor_scalar(dec_idx, dec_idx, 31, 31, ALU.logical_shift_left, ALU.arith_shift_right))
            ve.tensor_scalar(dec_m[2], dec_m[2], 8, None, ALU.bitwise_and)
            for j in range(1, 8):
                leaf(j)
            dve.wait_ge(dec_out, p * (16 * DEC_PER_PAIR) + 16 * (i + 1))
            done(leaf(0), apart=True)
            for b, n in ((0, 4), (1, 2), (2, 1)):
                pairs = dec_v[:, 0:8:8 // (2 * n), :].rearrange("p (n two) c -> p n two c", two=2)
                mask = dec_m[b].rearrange("p (n c) -> p n c", n=1).to_broadcast([P, n, DEC])
                ins = ve.copy_predicated(pairs[:, :, 0, :], mask, pairs[:, :, 1, :])
                if n > 1:
                    done(ins, apart=True)
            k[0] += 1
            assert k[0] == DEC_OPS
            ins.then_inc(dec_chain, 1)

        DEC_OPS = 6

        def rw_pool(pool, p, s):
            for m in range(RG):
                n = p * 16 + 2 * s + m
                pool.wait_ge(s_sb, n + 1)
                pool.wait_ge(r_sb, n + 1)
                ge.tensor_tensor(o_buf, o_buf, r_buf, ALU.mult).then_inc(o32_sb, 1)
                pool.wait_ge(o_hi, n + 1)
                ge.tensor_tensor(oT[s % 2][m][1], o_buf, oT[s % 2][m][0], ALU.subtract).then_inc(o_lo, 1)

        def split(pool, k, before, dst, nth, n=PW):
            wait_apart(pool, stg_full[k], 16 + before * 16)
            ge.tensor_scalar(dst[0], stg[:, k, 0:n], 1.0, 0.0, ALU.mult, ALU.add).then_inc(pool_chain, 1)
            pool.wait_ge(pool_chain, nth + 1)
            ge.tensor_tensor(dst[1], stg[:, k, 0:n], dst[0], ALU.subtract).then_inc(w_ready, 1)

        f32_buf = [w32(i * 512, 512) for i in range(2)]

        def ff_g(q, m, i):
            if q == 0:
                return w16(1024 + (m * 2 + i) * 256, 512)
            at = (m * 2 + i) // 3 * NTOK + (1 + (m * 2 + i) % 3) * CH
            return planes[:, 5, at:at + CH]

        gT = [[[ff_g(q, m, i) for i in range(2)] for m in range(4)] for q in range(2)]
        magic = 1.5 * 2.0 ** 23

        def ff_pe_proj(pe, p, s):
            g, c = s // 4, s % 4
            slot = weight_slot("ffn", g)
            if c == 0:
                pe.wait_ge(w_ready, p * 4 + WR_FF + 2 * g + 2)
            for m in range(4):
                n = p * 32 + 4 * s + m
                if not (isinstance(p, int) and s == 0):
                    pe.wait_ge(g32, n - 3)
                for kt in range(KT):
                    at = kt * CH + m * P
                    for x in range(2):
                        mm = te.matmul(ps[:, m, :], slot[:, at:at + P], tokT[x][:, kt, c * CH:c * CH + CH],
                                       start=(kt == 0 and x == 0), stop=(kt == KT - 1 and x == 1))
                mm.then_inc(h_ps, 1)

        def ff_pe_out(pe, p, s):
            slot = weight_slot("ffn", s // 4)
            pe.wait_ge(g_lo, p * 32 + 4 * s + 4)
            for j in range(TPC):
                out_tile(pe, O_FF + p * 32 + 4 * s + j, 6 + j % 2,
                         [(gT[s % 2][m][x][:, j * P:j * P + P], slot[:, PW + m * D:PW + m * D + D]) for m in range(4) for x in range(2)])

        def ff_act(act, p, s):
            g = s // 4
            if s % 4 == 0:
                act.wait_ge(par_cur, 2 * RW_PAIRS + p * 2 + g + 1)
            for m in range(4):
                n = p * 32 + 4 * s + m
                first = isinstance(p, int) and s == 0
                act.wait_ge(h_ps, n + 1)
                if not (first and m < 2):
                    act.wait_ge(g_lo, n - 1)
                se.activation(f32_buf[m % 2], ps[:, m, :], ACT.Gelu, bias=cur[:, g, m:m + 1]).then_inc(g32, 1)
                act.wait_ge(g32, n + 1)
                if m == 0 and not (isinstance(p, int) and s < 1):
                    act.wait_ge(wo_ps, O_FF + p * 32 + 4 * s)
                se.activation(gT[s % 2][m][0], f32_buf[m % 2], ACT.Copy).then_inc(g_hi, 1)

        def ff_dve(dve, p, s):
            g = s // 4
            if s % 4 == 0:
                if not (isinstance(p, int) and g == 0):
                    dve.wait_ge(g_hi, p * 32 + 4 * s)
                ve.tensor_copy(cur[:, g, 0:4], par[:, bass.ds(at_most(p * 8 + 4 * g, 12) + C_B1, 4)]).then_inc(par_cur, 1)
            for m in range(4):
                n = p * 32 + 4 * s + m
                dve.wait_ge(g_hi, n + 1)
                ve.tensor_tensor(gT[s % 2][m][1], f32_buf[m % 2], gT[s % 2][m][0], ALU.subtract).then_inc(g_lo, 1)

        def ff_dve_acc(dve, p, s):
            for j in range(TPC):
                accumulate(dve, O_FF + p * 32 + 4 * s + j, 6 + j % 2, (s % 4) * TPC + j)

        def ternary(pool, k, before, which, dst, nth):
            x = stg[:, k, :]
            pool.wait_ge(stg_full[k], 16 + before * 16)
            ge.tensor_scalar(x, x, wsc[:, 4 + which:5 + which], magic, ALU.mult, ALU.add).then_inc(pool_chain, 1)
            pool.wait_ge(pool_chain, nth * 2 + PC_FF + 1)
            ge.tensor_scalar(x, x, -magic, 1.0, ALU.add, ALU.mult).then_inc(pool_chain, 1)
            pool.wait_ge(pool_chain, nth * 2 + PC_FF + 2)
            ge.tensor_scalar(dst, x, 1.0, -1.0, ALU.min, ALU.max).then_inc(w_ready, 1)

        PC_FF = WR_FF
        PC_MO = PC_FF + 4 * F_GROUPS

        MU = LAYERS * NC
        vT = [[planes[:, 4, (q * 2 + i) * 2048:(q * 2 + i) * 2048 + 2048].rearrange("p (t d) -> p t d", t=TPC) for i in range(2)] for q in range(2)]
        oH = [[[planes[:, 5, ((q * 4 + j) * 2 + i) * 512:((q * 4 + j) * 2 + i) * 512 + 512] for i in range(2)] for j in range(4)] for q in range(2)]
        VB, OB, FB = 7, 6, 7

        def mo_u(p, s, j):
            return p * 32 + MU + 4 * s + j

        def mo_q(pe, p, s, j, which, between=None):
            g, c = s // 4, s % 4
            slot = weight_slot("moba", g)
            u = mo_u(p, s, j)
            pe_project(u, which, k_ps if which else q_ps,
                       lambda i, kt: halves(slot, which)[i][:, kt * CH + j * P:kt * CH + j * P + P],
                       lambda i, kt: tokT[i][:, kt, c * CH:c * CH + CH], between)

        def mo_v(pe, p, s, j):
            g, c = s // 4, s % 4
            slot = weight_slot("moba", g)
            if c == 0 and j == 0:
                pe.wait_ge(w_ready, p * 8 + WR_MO + 4 * g + 4)
            pe.wait_ge(mv_lo, p * 32 + 4 * s + j)
            if not (isinstance(p, int) and s == 0):
                pe.wait_ge(mw_acc, p * 32 + 4 * s + j)
            tt = c * TPC + j
            for kt in range(KT):
                for z, (x, y) in enumerate(PASSES):
                    mm = te.matmul(ps[:, VB, :], tokT[x][:, kt, tt * P:tt * P + P], halves(slot, 2)[y][:, kt * CH:kt * CH + CH],
                                   start=(kt == 0 and z == 0), stop=(kt == KT - 1 and z == 2))
            mm.then_inc(mv_ps, 1)

        def mo_out(pe, p, s, tt, prev_slot):
            pe.wait_ge(mo_lo, p * 32 + 4 * s)
            pe.wait_ge(mw_acc, p * 32 + 4 * s + tt + 4)
            q = (s - 1) % 2
            pairs = [(oH[q][j][x][:, tt * P:tt * P + P], halves(prev_slot, 3)[y][:, j * D:j * D + D]) for j in range(4) for x, y in PASSES]
            for z, (x, y) in enumerate(pairs):
                mm = te.matmul(ps[:, FB, :], x, y, start=(z == 0), stop=(z == len(pairs) - 1))
            mm.then_inc(mw_ps, 1)

        def mo_pv(pe, p, s, j):
            u = mo_u(p, s, j)
            pe.wait_ge(pT_split, u + 1)
            for b in range(2):
                for z, (x, y) in enumerate(PASSES):
                    te.matmul(ps[:, OB, b * S:b * S + S], vT[s % 2][x][:, 2 * b, j * P:j * P + P], pT[y][:, b * 384:b * 384 + S],
                              start=(z == 0), stop=False)
                for z, (x, y) in enumerate(PASSES):
                    mm = te.matmul(ps[:, OB, b * S + P:b * S + S], vT[s % 2][x][:, 2 * b + 1, j * P:j * P + P],
                                   pT[y][:, b * 384 + S:b * 384 + 384], start=False, stop=(z == 2))
            mm.then_inc(mo_ps, 1)

        def mo_rounds(eng, body):
            with eng.Fori(0, MO_PAIRS) as p:
                for s in range(8):
                    nstep = (p, s + 1) if s < 7 else (p + 1, 0)
                    cond = None if s < 7 else p < MO_PAIRS - 1
                    for j in range(4):
                        nround = (p, s, j + 1) if j < 3 else (*nstep, 0)
                        body(p, s, j, nround, nstep, cond if j == 3 else None, cond)

        def mo_pe(pe, p, s, j, nround, nstep, rcond, scond):
            u = mo_u(p, s, j)
            with Maybe(pe, rcond):
                mo_q(pe, *nround, 0)
            with Maybe(pe, scond):
                mo_v(pe, *nstep, j)
            if rcond is None:
                mo_q(pe, *nround, 1, lambda: pe_transpose_probs(pe, u))
            else:
                pe_transpose_probs(pe, u)
                with Maybe(pe, rcond):
                    mo_q(pe, *nround, 1)
            mo_pv(pe, p, s, j)
            with Maybe(pe, (p > 0) if s == 0 else None):
                if s < 7:
                    pe.wait_ge(mv_lo, p * 32 + 4 * (s + 1) + j + 1)
                else:
                    with Maybe(pe, scond):
                        pe.wait_ge(mv_lo, p * 32 + 4 * (s + 1) + j + 1)
                mo_out(pe, p, s, j, weight_slot("moba", ((s - 1) % 8) // 4))
            with Maybe(pe, rcond):
                pe_scores(pe, mo_u(*nround))

        def mo_act_v(act, p, s, j):
            n = p * 32 + 4 * s + j
            act.wait_ge(mv_ps, n + 1)
            se.activation(vT[s % 2][0][:, j, :], ps[:, VB, :], ACT.Copy).then_inc(mv_hi, 1)

        def mo_act(act, p, s, j, nround, nstep, rcond, scond):
            u = mo_u(p, s, j)
            with Maybe(act, rcond):
                act_q(act, mo_u(*nround))
            with Maybe(act, scond):
                mo_act_v(act, *nstep, j)
            act_pT(act, u)
            with Maybe(act, rcond):
                act_k(act, mo_u(*nround))
            n = p * 32 + 4 * s + j
            act.wait_ge(mo_ps, n + 1)
            se.activation(oH[s % 2][j][0], ps[:, OB, :], ACT.Copy).then_inc(mo_hi, 1)
            with Maybe(act, rcond):
                act_exp(act, mo_u(*nround))

        def mo_dve_v(dve, p, s, j):
            n = p * 32 + 4 * s + j
            dve.wait_ge(mv_hi, n + 1)
            ve.tensor_tensor(vT[s % 2][1][:, j, :], ps[:, VB, :], vT[s % 2][0][:, j, :], ALU.subtract).then_inc(mv_lo, 1)

        def mo_dve_acc(dve, p, s, tt):
            dve.wait_ge(mw_ps, p * 32 + 4 * s + tt + 5)
            x = h[:, ((s - 1) % 4) * TPC + tt, :]
            ve.tensor_tensor(x, ps[:, FB, :], x, ALU.add).then_inc(mw_acc, 1)

        def mo_dve(dve, p, s, j, nround, nstep, rcond, scond):
            u = mo_u(p, s, j)
            with Maybe(dve, rcond):
                dve_q(dve, mo_u(*nround))
            with Maybe(dve, scond):
                mo_dve_v(dve, *nstep, j)
            dve_pT(dve, u)
            with Maybe(dve, rcond):
                dve_k(dve, mo_u(*nround))
            n = p * 32 + 4 * s + j
            dve.wait_ge(mo_hi, n + 1)
            ve.tensor_tensor(oH[s % 2][j][1], ps[:, OB, :], oH[s % 2][j][0], ALU.subtract).then_inc(mo_lo, 1)
            with Maybe(dve, (p > 0) if s == 0 else None):
                mo_dve_acc(dve, p, s, j)
            with Maybe(dve, rcond):
                dve_max(dve, mo_u(*nround))
                dve_norm(dve, mo_u(*nround))

        GL_T = [(g, c) for g in range(3) for c in range(NC)]

        def gl_base(t):
            return sum(G_TILES[g] for g, _ in GL_T[:t])

        sg_buf = [w32(i * 512, 512) for i in range(2)]
        hT = [[[w16(1024 + ((q * 4 + m) * 2 + i) * 256, 512) for i in range(2)] for m in range(4)] for q in range(2)]

        def gl_rows(g, m):
            return G_LAST if g == 2 and m == 2 else P

        def gl_pe_proj(pe, t):
            g, c = GL_T[t]
            slot = weight_slot("glu", g)
            if c == 0:
                pe.wait_ge(w_ready, WR_GL + 3 * g + 3)
            for m in range(G_TILES[g]):
                n = gl_base(t) + m
                if n >= 2:
                    pe.wait_ge(prod_sb, n - 1)
                W = G_TILES[g] * P
                for piece, done in ((0, ga_ps), (1, up_ps)):
                    bank = 2 * (n % 2) + piece
                    for kt in range(KT):
                        for z, (i, j) in enumerate(PASSES):
                            at = kt * W + m * P
                            mm = te.matmul(ps[:, bank, :], halves(slot, piece)[i][:, at:at + P],
                                           tokT[j][:, kt, c * CH:c * CH + CH], start=(kt == 0 and z == 0),
                                           stop=(kt == KT - 1 and z == 2))
                    mm.then_inc(done, 1)

        def gl_pe_out(pe, t):
            g, c = GL_T[t]
            slot = weight_slot("glu", g)
            pe.wait_ge(gl_lo, gl_base(t + 1))
            for j in range(TPC):
                pairs = []
                for m in range(G_TILES[g]):
                    r = gl_rows(g, m)
                    pairs += [(hT[t % 2][m][x][0:r, j * P:j * P + P], halves(slot, 2)[y][0:r, m * D:m * D + D]) for x, y in PASSES]
                out_tile(pe, O_GL + 4 * t + j, 6 + j % 2, pairs)

        def gl_act(act, t):
            g, c = GL_T[t]
            for m in range(G_TILES[g]):
                n = gl_base(t) + m
                act.wait_ge(ga_ps, n + 1)
                if n >= 2:
                    act.wait_ge(gl_lo, n - 1)
                se.activation(sg_buf[n % 2], ps[:, 2 * (n % 2), :], ACT.Silu).then_inc(silu_sb, 1)
                act.wait_ge(prod_sb, n + 1)
                if m == 0 and t >= 2:
                    act.wait_ge(wo_ps, O_GL + 4 * t)
                se.activation(hT[t % 2][m][0], sg_buf[n % 2], ACT.Copy).then_inc(gl_hi, 1)

        def gl_dve(dve, t):
            g, c = GL_T[t]
            for m in range(G_TILES[g]):
                n = gl_base(t) + m
                dve.wait_ge(silu_sb, n + 1)
                dve.wait_ge(up_ps, n + 1)
                ve.tensor_tensor(sg_buf[n % 2], sg_buf[n % 2], ps[:, 2 * (n % 2) + 1, :], ALU.mult).then_inc(prod_sb, 1)
                dve.wait_ge(gl_hi, n + 1)
                ve.tensor_tensor(hT[t % 2][m][1], sg_buf[n % 2], hT[t % 2][m][0], ALU.subtract).then_inc(gl_lo, 1)

        def mix_act_copy(act, f, c, j):
            e = 16 * f + 4 * c + j
            act.wait_ge(ln_T, e + 1)
            if c == 0 and j == 0:
                act.wait_ge(setup_done, 1)
            if c > 0 and j == 0:
                act.wait_ge(mix_y, 12 * c)
            b, at = j // 2, 1 + (j % 2) * P
            src = ln_bank(e).rearrange("p (k t) -> p k t", k=KT)
            se.activation(xT32[:, :, b, at:at + P], src, ACT.Copy).then_inc(ln_done, 1)

        def mix_ops(c):
            return [(12 * c + 3 * kt + w, kt, w) for kt in range(KT) for w in range(3)]

        def mix_pool(pool, c):
            for e, kt, w in mix_ops(c):
                if e % 12 == 0:
                    pool.wait_ge(ln_done, 4 * c + 4)
                if e >= 2:
                    pool.wait_ge(mix_y, e - 1)
                col = (0, 4, 8)[w] + kt
                ge.tensor_scalar(mix_t[e % 2].rearrange("p (b t) -> p b t", b=2), xT32[:, kt, :, 0:256],
                                 mixc[:, col:col + 1], 0.0, ALU.mult, ALU.add).then_inc(mix_tmp, 1)
                if w == 1 and kt > 0:
                    mix_pool_lo(pool, e - 2)
            mix_pool_lo(pool, 12 * c + 11)

        def mix_dst(e, i):
            c, r = e // 12, e % 12
            return mix[r % 3][i][:, r // 3, c * CH:c * CH + CH]

        def mix_pool_lo(pool, e):
            pool.wait_ge(mix_hi, e + 1)
            ge.tensor_tensor(mix_dst(e, 1), mix_out[e % 3], mix_dst(e, 0), ALU.subtract).then_inc(mix_lo_v, 1)

        def mix_dve(dve, c):
            for e, kt, w in mix_ops(c):
                dve.wait_ge(mix_tmp, e + 1)
                if e >= 3:
                    if w < 2:
                        dve.wait_ge(mix_lo, (e - 3) // 3 * 2 + w + 1)
                    else:
                        dve.wait_ge(mix_lo_v, e // 3)
                col = (C_MR, C_MK, C_MV)[w] + kt
                ve.scalar_tensor_tensor(mix_out[e % 3].rearrange("p (b t) -> p b t", b=2), xT32[:, kt, :, 1:257],
                                        par[:, col:col + 1], mix_t[e % 2].rearrange("p (b t) -> p b t", b=2),
                                        ALU.mult, ALU.add).then_inc(mix_y, 1)
                if w == 2:
                    for x in (e - 2, e - 1):
                        dve.wait_ge(mix_hi, x + 1)
                        ve.tensor_tensor(mix_dst(x, 1), mix_out[x % 3], mix_dst(x, 0), ALU.subtract).then_inc(mix_lo, 1)

        def mix_act(act, c):
            for e, kt, w in mix_ops(c):
                act.wait_ge(mix_y, e + 1)
                se.activation(mix_dst(e, 0), mix_out[e % 3], ACT.Copy).then_inc(mix_hi, 1)

        def tok_pe(pe, l, c, nxt):
            u = l * 4 + c
            if nxt is not None:
                pe.wait_ge(to_free, 96 + 4 * c + 2 if isinstance(l, int) else u * 8 + 2)
                tok_project(pe, nxt[0], u + 1, nxt[1], 0, 0, q_ps)
                tok_project(pe, nxt[0], u + 1, nxt[1], 1, 1, k_ps)
            pe_transpose_probs(pe, u)
            if isinstance(l, int) and c > 0:
                ln_chunk(pe, ln_pe, 0, c - 1)
            if nxt is not None:
                pe_scores(pe, u + 1)
            if isinstance(l, int) and c > 0:
                pe.wait_ge(ln_done, 4 * c)
            tok_out_mm(pe, u, c, isinstance(l, int) and l == LAYERS - 1)

        def tok_act(act, l, c, nxt):
            u = l * 4 + c
            last = isinstance(l, int) and l == LAYERS - 1
            if nxt is not None:
                act_q(act, u + 1)
                act_k(act, u + 1)
            act_pT(act, u)
            if last and c > 0:
                ln_chunk(act, mix_act_copy, 0, c - 1)

            def out(n):
                act.wait_ge(to_ps, u * 8 + n + 1)
                se.activation(tok_dst(c, n, 0), ps[:, TOK_BANK[n], :], ACT.Copy).then_inc(to_hi, 1)

            if not last:
                out(0), out(1)
            if nxt is not None:
                act_exp(act, u + 1)
            if not last:
                for n in range(2, 8):
                    out(n)
            else:
                for n in range(4):
                    i = TOK_OUT[4 + n][1]
                    act.wait_ge(to_ps, 96 + 4 * c + n + 1)
                    se.activation(h[:, c * TPC + i, :], ps[:, TOK_BANK[n], :], ACT.Copy).then_inc(to_free, 1)
            if last and c > 0:
                mix_act(act, c - 1)
            if c < 2:
                act.wait_ge(stg_full[c], l * 16 + 16 * (P_ABS // 2 + 1))
                se.activation(stg[:, c, :], stg[:, c, :], ACT.Abs, accum_out=wabs(l, c)).then_inc(abs_done, 1)

        def wabs(l, k):
            return wsum[:, k * 4 + l:k * 4 + l + 1] if isinstance(l, int) else wsum[:, bass.ds(l + k * 4, 1)]

        def tok_dve(dve, l, c, nxt, chain):
            u = l * 4 + c
            last = isinstance(l, int) and l == LAYERS - 1
            if nxt is not None:
                dve_q(dve, u + 1)
                dve_k(dve, u + 1)
            if last and c > 0:
                ln_chunk(dve, ln_dve_x, 0, c - 1)
            dve_pT(dve, u)
            if nxt is not None:
                dve_max(dve, u + 1)

            def out(n):
                dve.wait_ge(to_hi, u * 8 + n + 1)
                ve.tensor_tensor(tok_dst(c, n, 1), ps[:, TOK_BANK[n], :], tok_dst(c, n, 0), ALU.subtract).then_inc(to_free, 1)

            if not last:
                for n in range(4):
                    out(n)
            if nxt is not None:
                dve_norm(dve, u + 1)
            if not last:
                for n in range(4, 8):
                    out(n)
            else:
                if c > 0:
                    mix_dve(dve, c - 1)
                dve.wait_ge(to_free, 4 + 96 + 4 * (c + 1))
                ln_dve_chunk(dve, 0, c, chain)

        def tower(eng, body, encode=None, before_last=None):
            with eng.Fori(0, LAYERS - 1) as l:
                for c in range(NC):
                    body(eng, l, c, (l, c + 1) if c < NC - 1 else (l + 1, 0))
                    if c < 2 and encode is not None:
                        with first_pair(eng, l):
                            encode(NC - 1, c)
            if before_last is not None:
                before_last()
            for c in range(NC):
                body(eng, LAYERS - 1, c, (LAYERS - 1, c + 1) if c < NC - 1 else None)

        def steps8(eng, pairs, own, nxt):
            with eng.Fori(0, pairs) as p:
                for s in range(8):
                    if s < 7:
                        nxt(eng, p, s + 1)
                    else:
                        with eng.If(p < pairs - 1):
                            nxt(eng, p + 1, 0)
                    own(eng, p, s)

        row = setup32[:, 0:D]
        peT = setup32[:, D:D + KT * S].rearrange("p (k t) -> p k t", k=KT)
        pe_rows = setup32[:, D + KT * S:D + KT * S + 2 * D].rearrange("p (a d) -> p a d", a=2)
        tok_cols = setup32[:, 2560:2560 + NTOK].bitcast(I32)
        tok_rows_i = setup32[:, 4608:4624].bitcast(I32)
        tok_rows = setup32[:, 4624:4640]
        ones = w32(7200, P)
        mask32 = work[:, 6000:6132]
        iota = work[:, 6128:6132]

        def enc_dst(e, half_):
            c, n = e // 8, e % 8
            return tokT[half_][:, n, c * CH:c * CH + CH] if n < 4 else encR(half_, c * TPC + n - 4)

        block = ctx.enter_context(nc.Block())

        @block.sync
        def _(sp):
            sp.dma_start(mask32, a["consts"][:, P:P + 132]).then_inc(consts_in, 16)
            sp.dma_start(setup32[:, 0:1536], a["consts"][:, K_ROW:K_ROW + 1536]).then_inc(consts_in, 16)
            sp.dma_start(tok_cols[:, 0:CH], a["tok_cols"][:, 0:CH]).then_inc(consts_in, 16)
            sp.dma_start(stg[:, 0, 0:1024], a["tok_w"][0]).then_inc(stg_full[0], 16)
            sp.dma_start(setup32[:, 1536:2560], a["consts"][:, K_ROW + 1536:K_ROW + 2560]).then_inc(rest_in, 16)
            sp.dma_start(tok_rows_i, a["tok_rows"]).then_inc(rest_in, 16)
            sp.dma_start(ident[:, :], a["consts"][:, 0:P]).then_inc(rest_in, 16)
            sp.dma_start(par[:, :], a["par"]).then_inc(rest_in, 16)
            sp.dma_start(tok_cols[:, CH:NTOK], a["tok_cols"][:, CH:NTOK]).then_inc(rest_in, 16)
            for i in range(1, LAYERS):
                if i >= 2:
                    sp.wait_ge(w_ready, i - 1)
                sp.dma_start(stg[:, i % 2, 0:1024], a["tok_w"][i]).then_inc(stg_full[i % 2], 16)
            for i in range(2 * F_GROUPS):
                if i < 2:
                    sp.wait_ge(w_ready, LAYERS - 1 + i)
                else:
                    sp.wait_ge(abs_done, i - 1)
                sp.dma_start(stg[:, i % 2, :], a["ff_w"][i]).then_inc(stg_full[i % 2], 16)
            for i in range(4):
                if i < 2:
                    sp.wait_ge(abs_done, 2 * F_GROUPS - 1 + i)
                else:
                    sp.wait_ge(w_ready, WR_RW + i - 1)
                sp.dma_start(stg[:, i % 2, :], a["rw_w"][i]).then_inc(stg_full[i % 2], 16)
            sp.wait_ge(mix_lo, 8 * NC)
            sp.wait_ge(mix_lo_v, 4 * NC)
            sp.dma_start(dec_idx, a["glu_idx"][:, 0:DEC]).then_inc(idx_in, 16)
            with sp.Fori(0, RW_PAIRS) as p:
                def rw_piece(k):
                    wait_apart(sp, w_ready, p * 4 + WR_RW + 4 + k - 1)
                    with last_pair(sp, p, RW_PAIRS):
                        sp.dma_start(stg[:, k % 2, :], a["ff_w"][k]).then_inc(stg_full[k % 2], 16)
                    with sp.If(p < RW_PAIRS - 1):
                        sp.dma_start(stg[:, k % 2, :], a["rw_w"][bass.ds(at_most(p * 4 + 4 + k, 2 * R_GROUPS - 1), 1)].rearrange("a p n -> (a p) n")).then_inc(stg_full[k % 2], 16)

                def dec_done(i, k):
                    wait_apart(sp, dec_chain, p * (DEC_PER_PAIR * DEC_OPS) + i * DEC_OPS + k + 1)

                def load_idx(pp, i):
                    sp.dma_start(dec_idx, a["glu_idx"][:, bass.ds(at_most(pp * (DEC_PER_PAIR * DEC) + i * DEC, G_COLS - DEC), DEC)]).then_inc(idx_in, 16)

                for i in range(DEC_PER_PAIR):
                    dec_done(i, 3)
                    if i < DEC_PER_PAIR - 1:
                        load_idx(p, i + 1)
                    else:
                        with sp.If(p < RW_PAIRS - 1):
                            load_idx(p + 1, 0)
                    dec_done(i, DEC_OPS)
                    sp.dma_start(dec_dram[:, bass.ds(p * (DEC_PER_PAIR * DEC) + i * DEC, DEC)], dec_v[:, 0, :]).then_inc(dec_out, 16)
                    if i in (3, 5, 11, 13):
                        rw_piece((3, 5, 11, 13).index(i))
            sp.wait_ge(dec_chain, DEC_BLOCKS * DEC_OPS + 1)
            sp.dma_start(b2row, a["b2"]).then_inc(b2_in, 16)
            with sp.Fori(2, F_GROUPS) as q:
                for k in range(2):
                    wait_apart(sp, w_ready, q * 2 + WR_FF + k - 1)
                    sp.dma_start(stg[:, k, :], a["ff_w"][bass.ds(q * 2 + k, 1)].rearrange("a p n -> (a p) n")).then_inc(stg_full[k], 16)
            with sp.Fori(0, 2 * M_GROUPS) as q:
                for k in range(2):
                    wait_apart(sp, w_ready, q * 2 + WR_MO + k - 1)
                    sp.dma_start(stg[:, k, :], a["mo_w"][bass.ds(q * 2 + k, 1)].rearrange("a p n -> (a p) n")).then_inc(stg_full[k], 16)
            sp.wait_ge(dec_out, 16 * DEC_BLOCKS + 16)
            at = 0
            for i in range(9):
                n = (G_WIDTH if i % 3 < 2 else D_WIDTH)[i // 3]
                sp.wait_ge(w_ready, WR_GL + i - 1)
                sp.dma_start(stg[:, i % 2, 0:n], dec_dram[:, at:at + n]).then_inc(stg_full[i % 2], 16)
                at += n
            for c in range(NC):
                sp.wait_ge(wo_acc, 2 + O_GL + 4 * (2 * NC + c) + 4)
                sp.dma_start(a["out"][:, c * TPC:c * TPC + TPC, :], h[:, c * TPC:c * TPC + TPC, :]).then_inc(out_sem, 16)
            sp.wait_ge(out_sem, 16 * NC)

        @block.gpsimd
        def _(pool):
            def tok_split(i):
                split(pool, i % 2, i // 2, [wa[:, 8192 + x * 4096 + i * 1024:8192 + x * 4096 + i * 1024 + 1024] for x in range(2)], i, 1024)

            def enc_low_rows(c):
                for n in range(TPC):
                    e = 8 * c + 4 + n
                    pool.wait_ge(enc_hi, e + 1)
                    ge.tensor_tensor(enc_dst(e, 1), tok_tmp[e % 4], enc_dst(e, 0), ALU.subtract).then_inc(enc_lo_rows, 1)

            tok_split(0), enc_low_rows(0), enc_low_rows(1), tok_split(1), tok_split(2)
            enc_low_rows(2), tok_split(3), enc_low_rows(3)

            def rw_split(g, pp, k):
                slot = weight_slot("rwkv", g)
                idx = pp * 4 + (2 * g + k + WR_RW)
                before = pp * 2 + (P_RW // 2 + g)
                split(pool, k, before, halves(slot, k), idx)

            for c in range(NC):
                ln_pool_chunk(pool, 0, c)
                if c in (1, 2):
                    rw_split(0, 0, c - 1)
                mix_pool(pool, c)
            pool.wait_ge(k_ps, MU)
            rw_split(1, 0, 0), rw_split(1, 0, 1)

            def ffn_piece(g, k):
                pool.wait_ge(scale_done, 1)
                dst = weight_slot("ffn", g)[:, k * PW:k * PW + PW]
                ternary(pool, k, P_FF // 2 + g, k, dst, 2 * g + k)

            with pool.Fori(0, RW_PAIRS) as p:
                for s in range(8):
                    rw_pool(pool, p, s)
                    if s >= 5:
                        with last_pair(pool, p, RW_PAIRS):
                            ln_pool_chunk(pool, 1, s - 5)
                    if s in (1, 2):
                        with pool.If(p > 0):
                            pool.wait_ge(wo_ps, p * 32 + 4)
                            rw_split(1, p, s - 1)
                    if s in (5, 6):
                        with pool.If(p < RW_PAIRS - 1):
                            pool.wait_ge(wo_ps, p * 32 + 20)
                            rw_split(0, p + 1, s - 5)
                        with last_pair(pool, p, RW_PAIRS):
                            pool.wait_ge(wo_ps, O_FF - 12)
                            ffn_piece(0, s - 5)

            def mo_w(g):
                for k in range(4):
                    split(pool, k % 2, P_MO // 2 + 2 * g + k // 2, halves(weight_slot("moba", g), k), PC_MO + 4 * g + k)

            ln_pool_chunk(pool, 1, NC - 1)
            for g in range(1, F_GROUPS):
                pool.wait_ge(wo_ps, O_FF + 4 + 16 * (g - 1))
                ffn_piece(g, 0), ffn_piece(g, 1)
            mo_w(0)
            for c in range(NC):
                ln_pool_chunk(pool, 2, c)
            mo_w(1)
            for g in (2, 3):
                pool.wait_ge(mw_ps, 8 + 16 * (g - 1))
                mo_w(g)

            def gl_w(g):
                for k in range(3):
                    i = 3 * g + k
                    n = (G_WIDTH if k < 2 else D_WIDTH)[g]
                    split(pool, i % 2, (P_GL + i) // 2, halves(weight_slot("glu", g), k, n), PC_MO + 16 + i, n)

            pool.wait_ge(mw_ps, 8 + 48)
            gl_w(0)
            for c in range(NC):
                ln_pool_chunk(pool, 3, c)
            gl_w(1)
            pool.wait_ge(wo_ps, O_GL + 20)
            gl_w(2)

        @block.scalar
        def _(act):
            def encode(c, part):
                for e in range(8 * c + 4 * part, 8 * c + 4 * part + 4):
                    act.wait_ge(enc32, e + 1)
                    se.activation(enc_dst(e, 0), tok_tmp[e % 4], ACT.Copy).then_inc(enc_hi, 1)

            encode(0, 0), encode(0, 1), encode(1, 0), encode(1, 1)
            act_q(act, 0)
            act_k(act, 0)
            encode(2, 0), encode(2, 1)
            act_exp(act, 0)
            tower(act, tok_act, encode)
            ln_chunk(act, mix_act_copy, 0, NC - 1)
            mix_act(act, NC - 1)
            se.activation(wtmp[:, :], par[:, C_DECAY:C_DECAY + HEADS], ACT.Exp).then_inc(act_chain, 1)
            act.wait_ge(act_chain, 1)
            se.activation(wdec[:, :], wtmp[:, :], ACT.Exp, scale=-1.0).then_inc(act_chain, 1)
            rw_act(act, 0, 0)
            with act.Fori(0, RW_PAIRS) as p:
                for s in range(8):
                    if s < 7:
                        rw_act(act, p, s + 1)
                    else:
                        with act.If(p < RW_PAIRS - 1):
                            rw_act(act, p + 1, 0)
            ln_chunk(act, ln_act, 1, 0)
            ff_act(act, 0, 0)
            ln_chunk(act, ln_act, 1, 1)
            with act.Fori(0, FF_PAIRS) as p:
                for s in range(8):
                    if s < 7:
                        ff_act(act, p, s + 1)
                        if s < 2:
                            with first_pair(act, p):
                                ln_chunk(act, ln_act, 1, s + 2)
                    else:
                        with act.If(p < FF_PAIRS - 1):
                            ff_act(act, p + 1, 0)
            ln_chunk(act, ln_act, 2, 0)
            for j in range(TPC):
                mo_act_v(act, 0, 0, j)
            ln_chunk(act, ln_act, 2, 1)
            act_q(act, MU)
            act_k(act, MU)
            ln_chunk(act, ln_act, 2, 2)
            ln_chunk(act, ln_act, 2, 3)
            act_exp(act, MU)
            mo_rounds(act, lambda *x: mo_act(act, *x))
            ln_chunk(act, ln_act, 3, 0)
            for t in range(len(GL_T)):
                gl_act(act, t)
                if t < NC - 1:
                    ln_chunk(act, ln_act, 3, t + 1)

        @block.vector
        def _(dve):
            k = [0]

            def chain(ins):
                k[0] += 1
                ins.then_inc(dve_chain, 1)
                dve.wait_ge(dve_chain, k[0])

            ve.memset(ones, 1.0).then_inc(to_free, 4)
            ve.memset(wsum[:, :], 0.0).then_inc(wo_ps, 4)
            ve.memset(half[:, :], -0.5).then_inc(wo_acc, 2)
            ve.memset(rsum[:, :], 0.0).then_inc(dec_out, 16)
            ve.memset(stat[:, :, :], 0.0).then_inc(dec_chain, 1)
            ve.memset(mv[:, :, :], 0.0).then_inc(mw_ps, 8)
            ve.memset(rstd[:, :], 0.0).then_inc(mw_acc, 8)

            def setup():
                dve.wait_ge(rest_in, 80)
                lut = par[:, C_LUT:C_LUT + 16].bitcast(I32).rearrange("p (j b) -> p j b", b=2)
                ve.tensor_tensor(lutx[:, :], lut[:, :, 0], lut[:, :, 1], ALU.bitwise_xor)
                ve.tensor_copy(identb[:, :], ident[:, :])
                ve.tensor_copy(maskb[:, :], mask32[:, 0:P])
                ve.tensor_scalar(mixc[:, :], par[:, 0:12], -1.0, 1.0, ALU.mult, ALU.add)
                chain(ve.tensor_copy(tok_rows, tok_rows_i))

            def enc_low(e):
                dve.wait_ge(enc_hi, e + 1)
                ve.tensor_tensor(enc_dst(e, 1), tok_tmp[e % 4], enc_dst(e, 0), ALU.subtract).then_inc(enc_lo, 1)

            def encode(c, part):
                for e in range(8 * c + 4 * part, 8 * c + 4 * part + 4):
                    n = e % 8
                    if e == 4:
                        setup()
                    if e >= 4:
                        dve.wait_ge(enc_lo if n >= 4 else enc_lo_rows, (e - 4) // 8 * 4 + (e - 4) % 4 + 1)
                    if n < 4:
                        for b in range(2):
                            ins = ve.scalar_tensor_tensor(tok_tmp[e % 4][:, b * S:b * S + S], tok_cols[:, c * CH + b * S:c * CH + b * S + S],
                                                          iota[:, n:n + 1], peT[:, n, :], ALU.is_equal, ALU.add)
                    else:
                        tt = c * TPC + n - 4
                        ins = ve.scalar_tensor_tensor(tok_tmp[e % 4], row, tok_rows[:, tt:tt + 1], pe_rows[:, tt % 2, :],
                                                      ALU.is_equal, ALU.add)
                    ins.then_inc(enc32, 1)
                    if 0 < n < 4:
                        enc_low(e - 1)
                if part == 0:
                    enc_low(8 * c + 3)

            dve.wait_ge(consts_in, 48)
            encode(0, 0), encode(0, 1), encode(1, 0), encode(1, 1)
            dve_q(dve, 0)
            dve_k(dve, 0)
            encode(2, 0), encode(2, 1)
            dve_max(dve, 0)
            dve_norm(dve, 0)
            tower(dve, lambda *x: tok_dve(*x, chain), encode,
                  lambda: ve.memset(xT32[:, :, :, 0:1], 0.0).then_inc(setup_done, 1))
            dve.wait_ge(wsum_ps, 1)
            chain(ve.tensor_reduce(wsc[:, 0:2], ps[:, 7, 0:8].rearrange("p (w g) -> p w g", w=2), AX.X, ALU.add))
            chain(ve.tensor_scalar(wsc[:, 2:4], wsc[:, 0:2], 1.0 / (FF * D), 1e-8, ALU.mult, ALU.max))
            ve.reciprocal(wsc[:, 4:6], wsc[:, 2:4]).then_inc(scale_done, 1)
            ln_chunk(dve, ln_dve_x, 0, NC - 1)
            mix_dve(dve, NC - 1)
            for b in range(2):
                for x in (kv_buf, s_buf):
                    ins = ve.memset(x[:, b, 0:1], 0.0)
            dve.wait_ge(act_chain, 2)
            for m in range(RG):
                rw_dve(dve, 0, 0, m)
            with dve.Fori(0, RW_PAIRS) as p:
                for s in range(8):
                    for m in range(RG):
                        if s < 7:
                            rw_dve(dve, p, s + 1, m)
                        else:
                            with dve.If(p < RW_PAIRS - 1):
                                rw_dve(dve, p + 1, 0, m)
                            with last_pair(dve, p, RW_PAIRS):
                                if m == 0:
                                    ln_chunk(dve, ln_dve_lo, 1, 0)
                                    ln_chunk(dve, ln_dve_x, 1, 1)
                                    dec_block(dve, RW_PAIRS - 1, 13)
                                else:
                                    dve.wait_ge(o_lo, 8 * NC * RG)
                                    ff_dve(dve, 0, 0)
                                    ln_chunk(dve, ln_dve_lo, 1, 1)
                                    ln_chunk(dve, ln_dve_x, 1, 2)
                        if m == 0:
                            if s < 7:
                                rw_dve_acc(dve, p, s, 0)
                                if s == 6:
                                    with last_pair(dve, p, RW_PAIRS):
                                        ln_chunk(dve, ln_dve_x, 1, 0)
                                dec_block(dve, p, 2 * s)
                            else:
                                with dve.If(p < RW_PAIRS - 1):
                                    rw_dve_acc(dve, p, s, 0)
                                    dec_block(dve, p, 2 * s)
                                with last_pair(dve, p, RW_PAIRS):
                                    rw_dve_acc(dve, p, s, 0)
                    rw_dve_acc(dve, p, s, 1)
                    if s >= 4:
                        with last_pair(dve, p, RW_PAIRS):
                            dve.wait_ge(wo_acc, 2 + O_FF - 12 + 4 * (s - 4))
                            ln_dve_chunk(dve, 1, s - 4, chain)
                    if s < 6:
                        dec_block(dve, p, 2 * s + 1)
                    else:
                        with dve.If(p < RW_PAIRS - 1):
                            dec_block(dve, p, 2 * s + 1)

            with dve.Fori(0, FF_PAIRS) as p:
                for s in range(8):
                    if s < 7:
                        ff_dve(dve, p, s + 1)
                        if s < 2:
                            with first_pair(dve, p):
                                ln_chunk(dve, ln_dve_lo, 1, s + 2)
                                if s == 0:
                                    ln_chunk(dve, ln_dve_x, 1, 3)
                    else:
                        with dve.If(p < FF_PAIRS - 1):
                            ff_dve(dve, p + 1, 0)
                    ff_dve_acc(dve, p, s)
                    if s in (2, 3):
                        with first_pair(dve, p):
                            dec_block(dve, RW_PAIRS - 1, 12 + s)
                    if s >= 4:
                        with first_pair(dve, p):
                            dve.wait_ge(b2_in, 16)
                            dve.wait_ge(wo_acc, 2 + O_FF + 4 * (s + 1))
                            for tt in range((s - 4) * TPC, (s - 3) * TPC):
                                ins = ve.tensor_tensor(h[:, tt, :], h[:, tt, :], b2row, ALU.add)
                            ins.then_inc(b2_added, 1)
                            dve.wait_ge(b2_added, s - 3)
                        with last_pair(dve, p, FF_PAIRS):
                            dve.wait_ge(wo_acc, 2 + O_GL - 12 + 4 * (s - 4))
                            ln_dve_chunk(dve, 2, s - 4, chain)

            def mo_dve_round(p, s, j, *rest):
                mo_dve(dve, p, s, j, *rest)
                if s >= 5 and j == 3:
                    with last_pair(dve, p, MO_PAIRS):
                        dve.wait_ge(mw_acc, 8 + 52 + 4 * (s - 5))
                        ln_dve_chunk(dve, 3, s - 5, chain)

            ln_chunk(dve, ln_dve_x, 2, 0)
            ln_chunk(dve, ln_dve_lo, 2, 0)
            ln_chunk(dve, ln_dve_x, 2, 1)
            for j in range(TPC):
                mo_dve_v(dve, 0, 0, j)
            ln_chunk(dve, ln_dve_lo, 2, 1)
            ln_chunk(dve, ln_dve_x, 2, 2)
            dve_q(dve, MU)
            dve_k(dve, MU)
            ln_chunk(dve, ln_dve_lo, 2, 2)
            ln_chunk(dve, ln_dve_x, 2, 3)
            ln_chunk(dve, ln_dve_lo, 2, 3)
            dve_max(dve, MU)
            dve_norm(dve, MU)
            mo_rounds(dve, mo_dve_round)
            ln_chunk(dve, ln_dve_x, 3, 0)
            for tt in range(TPC):
                mo_dve_acc(dve, MO_PAIRS, 0, tt)
            ln_chunk(dve, ln_dve_lo, 3, 0)
            dve.wait_ge(mw_acc, 8 + 64)
            ln_dve_chunk(dve, 3, 3, chain)
            ln_chunk(dve, ln_dve_x, 3, 1)
            for t in range(len(GL_T)):
                gl_dve(dve, t)
                if t < NC - 1:
                    ln_chunk(dve, ln_dve_lo, 3, t + 1)
                if t < NC - 2:
                    ln_chunk(dve, ln_dve_x, 3, t + 2)
                if t > 0:
                    for j in range(TPC):
                        accumulate(dve, O_GL + 4 * (t - 1) + j, 6 + j % 2, GL_T[t - 1][1] * TPC + j)
            for j in range(TPC):
                accumulate(dve, O_GL + 44 + j, 6 + j % 2, 12 + j)

        @block.tensor
        def _(pe):
            tok_project(pe, 0, 0, 0, 0, 0, q_ps)
            tok_project(pe, 0, 0, 0, 1, 1, k_ps)
            pe_scores(pe, 0)
            tower(pe, tok_pe)
            pe.wait_ge(abs_done, 2 * F_GROUPS)
            pe.wait_ge(to_free, 4 + 96 + 16)
            te.matmul(ps[:, 7, 0:8], ones, wsum[:, :], start=True, stop=True).then_inc(wsum_ps, 1)
            pe.wait_ge(mix_lo, 8)
            pe.wait_ge(mix_lo_v, 4)
            rw_pe_proj(pe, 0, 0, 0), rw_pe_proj(pe, 0, 0, 1)
            pe.wait_ge(scale_done, 1)
            ln_chunk(pe, ln_pe, 0, NC - 1)
            pe.wait_ge(mix_lo, 8 * NC)
            pe.wait_ge(mix_lo_v, 4 * NC)

            with pe.Fori(0, RW_PAIRS) as p:
                for s in range(8):
                    for m in range(RG):
                        if s < 7:
                            rw_pe_proj(pe, p, s + 1, m)
                        else:
                            with pe.If(p < RW_PAIRS - 1):
                                rw_pe_proj(pe, p + 1, 0, m)
                            with last_pair(pe, p, RW_PAIRS):
                                if m == 0:
                                    pe.wait_ge(r_sb, NC * HEADS)
                                    pe.wait_ge(k_sb, NC * HEADS)
                                    pe.wait_ge(kv_sb, NC * HEADS)
                                ln_chunk(pe, ln_pe, 1, m)
                                if m == 0:
                                    pe.wait_ge(ln_done, 20)
                                    ff_pe_proj(pe, 0, 0)
                        rw_pe_out(pe, p, s, m)

            def ff_pe_next(pe, p, s):
                if 1 <= s < NC:
                    with first_pair(pe, p):
                        pe.wait_ge(ln_done, 16 + 4 * (s + 1))
                ff_pe_proj(pe, p, s)
                if 1 <= s < NC - 1:
                    with first_pair(pe, p):
                        ln_chunk(pe, ln_pe, 1, s + 1)

            steps8(pe, FF_PAIRS, ff_pe_out, ff_pe_next)
            ln_chunk(pe, ln_pe, 2, 0)
            pe.wait_ge(ln_done, 36)
            for j in range(TPC):
                mo_v(pe, 0, 0, j)
            ln_chunk(pe, ln_pe, 2, 1)
            mo_q(pe, 0, 0, 0, 0)
            mo_q(pe, 0, 0, 0, 1)
            ln_chunk(pe, ln_pe, 2, 2)
            ln_chunk(pe, ln_pe, 2, 3)
            pe.wait_ge(ln_done, 48)
            pe_scores(pe, MU)
            mo_rounds(pe, lambda *x: mo_pe(pe, *x))
            for tt in range(TPC):
                mo_out(pe, MO_PAIRS, 0, tt, weight_slot("moba", 1))
            ln_chunk(pe, ln_pe, 3, 0)
            pe.wait_ge(ln_done, 52)
            gl_pe_proj(pe, 0)
            ln_chunk(pe, ln_pe, 3, 1)
            for t in range(len(GL_T)):
                if t < len(GL_T) - 1:
                    if t + 1 < NC:
                        pe.wait_ge(ln_done, 48 + 4 * (t + 2))
                    gl_pe_proj(pe, t + 1)
                if t + 2 < NC:
                    ln_chunk(pe, ln_pe, 3, t + 2)
                gl_pe_out(pe, t)


def kernel(**inputs):
    import numpy as np
    import concourse.bacc as bacc
    from concourse.bass_utils import run_bass_kernel_spmd

    x = np.asarray(inputs["x"])
    W = {k: np.asarray(v) for k, v in inputs.items()}

    def rows(w, n):
        return w.reshape(-1, P, n).transpose(1, 0, 2)

    def flat(*parts):
        return np.concatenate([p.reshape(P, -1) for p in parts], axis=1)

    def pad(w, n, axis):
        out = np.zeros([n if i == axis else s for i, s in enumerate(w.shape)], w.dtype)
        out[(slice(None),) * axis + (slice(0, w.shape[axis]),)] = w
        return out

    tok_w = np.stack([flat(rows(W["L0_tok_Wq"][i], P), rows(W["L0_tok_Wk"][i], P)) for i in range(LAYERS)])
    r, k, v = (W["L0_attn_" + n].T for n in ("Wr", "Wk", "Wv"))
    o = W["L0_attn_Wo"].T
    n = RG * P
    rw_w = np.stack([q for g in range(R_GROUPS) for q in (
        flat(rows(r[:, g * n:g * n + n], n), rows(k[:, g * n:g * n + n], n)),
        flat(rows(v[:, g * n:g * n + n], n), rows(o[g * n:g * n + n], D)))])
    w1, w2 = W["L0_ffn_w1"].T, W["L0_ffn_w2"].T
    ff_w = np.stack([q for g in range(F_GROUPS) for q in (
        flat(rows(w1[:, g * CH:g * CH + CH], CH)), flat(rows(w2[g * CH:g * CH + CH], D)))])
    mq, mk, mvv, mo = (W["L1_attn_" + n] for n in ("Wq", "Wk", "Wv", "Wo"))
    mo_w = np.stack([q for g in range(M_GROUPS) for q in (
        *(flat(rows(w[:, g * CH:g * CH + CH], CH)) for w in (mq, mk, mvv)), flat(rows(mo[g * CH:g * CH + CH], D)))])
    full = sum(G_TILES) * P
    gi, ui = (pad(W[n].T, full, 1) for n in ("L1_ffn_gate_idx", "L1_ffn_up_idx"))
    di = pad(W["L1_ffn_down_idx"].T, full, 0)
    parts, at = [], 0
    for t in G_TILES:
        parts += [rows(gi[:, at:at + t * P], t * P), rows(ui[:, at:at + t * P], t * P), rows(di[at:at + t * P], D)]
        at += t * P
    glu_idx = flat(*parts)

    def cols(w):
        return w.reshape(-1, P).T

    par = flat(cols(W["L0_attn_time_mix_r"]), cols(W["L0_attn_time_mix_k"]), cols(W["L0_attn_time_mix_v"]),
               cols(W["L0_attn_time_decay"]), cols(W["L0_attn_time_first"]), cols(W["L0_ffn_b1"]),
               np.broadcast_to(W["L1_ffn_lut"], (P, 16)))

    f = np.float32
    pos = np.arange(S, dtype=f)[:, None]
    div = np.exp(-(np.log(f(10000.0)) / f(D)) * np.arange(0, D, 2, dtype=f))
    enc = np.zeros((S, D), f)
    enc[:, 0::2] = np.sin(pos * div)
    enc[:, 1::2] = np.cos(pos * div)
    i = np.arange(P)
    consts = np.concatenate([
        np.eye(P, dtype=f), np.where(i[None, :] > i[:, None], f(-1e30), f(0)),
        (i[:, None] + P * np.arange(KT)[None, :]).astype(f),
        np.broadcast_to(np.arange(D, dtype=f), (P, D)), flat(rows(enc.T, S)), flat(rows(enc, D))], axis=1)

    arrays = {
        "tok_cols": np.broadcast_to(x.reshape(1, NTOK), (P, NTOK)), "tok_rows": x.reshape(NT, P).T, "consts": consts, "par": par,
        "b2": np.broadcast_to(W["L0_ffn_b2"], (P, D)), "tok_w": tok_w, "rw_w": rw_w, "ff_w": ff_w, "mo_w": mo_w, "glu_idx": glu_idx,
    }
    arrays = {name: np.ascontiguousarray(v) for name, v in arrays.items()}
    nc = bacc.Bacc("TRN2", target_bir_lowering=False, num_devices=1)
    a = {name: nc.dram_tensor("in_" + name, v.shape, mybir.dt.from_np(v.dtype), kind="ExternalInput").ap() for name, v in arrays.items()}
    a["glu_dec"] = nc.dram_tensor("glu_dec", (P, G_COLS), F32, kind="Internal").ap()
    out = nc.dram_tensor("out", (B, S, D), F32, kind="ExternalOutput").ap()
    a["out"] = out.rearrange("b s d -> (b s) d").rearrange("(t p) d -> p t d", p=P)
    build(nc, a)
    got = run_bass_kernel_spmd(nc, [{"in_" + name: v for name, v in arrays.items()}], core_ids=[0])
    return got.results[0]["out"]
```
